# Optimizing a Trainium2 kernel written in Bass

```python
import numpy as np
import jax
import jax.numpy as jnp

def _softmax(x, axis=-1):
    return jax.nn.softmax(x, axis=axis)

def _gelu(x):
    return jax.nn.gelu(x, approximate=True)

def _silu(x):
    return jax.nn.silu(x)

def _sigmoid(x):
    return jax.nn.sigmoid(x)

def _layernorm(x, axis=-1, eps=1e-05):
    m = jnp.mean(x, axis=axis, keepdims=True)
    v = jnp.var(x, axis=axis, keepdims=True)
    return (x - m) / jnp.sqrt(v + eps)

def _scatter_add(tgt, idx, src, axis=0):
    return tgt.at[idx].add(src)

def _segment_sum(src, seg, n):
    return jax.ops.segment_sum(src, seg, n)
kernel_name = 'mk_cond_seq_d2_seqx_r4_137086'

def setup_inputs(seed: int=0):
    np.random.seed(seed)
    _w = jnp.asarray

    def _rec_inputs():
        import jax
        import jax.numpy as jnp
        _rk = jax.random.key(seed)
        x = 1.648e-05 + 1 * jax.random.normal(jax.random.fold_in(_rk, 1), (8, 256, 288), jnp.float32)
        _lenS = 256 - jax.random.randint(jax.random.fold_in(_rk, 7), (8,), 0, max(1, 256 // 4) + 1, jnp.int32)
        _lenS2 = 256 - jax.random.randint(jax.random.fold_in(_rk, 8), (8,), 0, max(1, 256 // 4) + 1, jnp.int32)
        cond_1152 = 0.00914911 + 1.00357 * jax.random.normal(jax.random.fold_in(_rk, 11), (8, 288), jnp.float32)
        return (x, cond_1152)
    x, cond_1152 = _rec_inputs()

    def _L0_cond_setup():
        import jax, jax.numpy as jnp
        import numpy as np
        B, N, D = (8, 256, 288)
        H = 16
        HD = D // H
        HID = 4 * D
        EPS = 1e-06

        def _ln(x):
            mu = jnp.mean(x, axis=-1, keepdims=True)
            var = jnp.mean(jnp.square(x - mu), axis=-1, keepdims=True)
            return (x - mu) * jax.lax.rsqrt(var + EPS)

        def _modulate(x, shift, scale):
            return x * (1.0 + scale[:, None, :]) + shift[:, None, :]

        def _attn(x, w_qkv, b_qkv, w_proj, b_proj):
            b, n, d = x.shape
            qkv = (x @ w_qkv + b_qkv).reshape(b, n, 3, H, HD)
            q = qkv[:, :, 0].transpose(0, 2, 1, 3)
            k = qkv[:, :, 1].transpose(0, 2, 1, 3)
            v = qkv[:, :, 2].transpose(0, 2, 1, 3)
            scores = jnp.einsum('bhnd,bhmd->bhnm', q, k) * HD ** (-0.5)
            attn = jax.nn.softmax(scores, axis=-1)
            out = jnp.einsum('bhnm,bhmd->bhnd', attn, v)
            out = out.transpose(0, 2, 1, 3).reshape(b, n, d)
            return out @ w_proj + b_proj
        key = jax.random.key(seed)
        ks = jax.random.split(key, 12)
        s = 0.02
        return {'x': jax.random.normal(ks[0], (B, N, D), jnp.float32), 't_emb': jax.random.normal(ks[1], (B, D), jnp.float32), 'w_qkv': jax.random.normal(ks[2], (D, 3 * D), jnp.float32) * s, 'b_qkv': jax.random.normal(ks[3], (3 * D,), jnp.float32) * s, 'w_proj': jax.random.normal(ks[4], (D, D), jnp.float32) * s, 'b_proj': jax.random.normal(ks[5], (D,), jnp.float32) * s, 'w_fc1': jax.random.normal(ks[6], (D, HID), jnp.float32) * s, 'b_fc1': jax.random.normal(ks[7], (HID,), jnp.float32) * s, 'w_fc2': jax.random.normal(ks[8], (HID, D), jnp.float32) * s, 'b_fc2': jax.random.normal(ks[9], (D,), jnp.float32) * s, 'w_ada': jax.random.normal(ks[10], (D, 6 * D), jnp.float32) * s, 'b_ada': jax.random.normal(ks[11], (6 * D,), jnp.float32) * s}
    _L0_cond_all = _L0_cond_setup()
    _L0_cond_in = {k: v for k, v in _L0_cond_all.items() if k in ('w_qkv', 'b_qkv', 'w_proj', 'b_proj', 'w_fc1', 'b_fc1', 'w_fc2', 'b_fc2', 'w_ada', 'b_ada')}
    del _L0_cond_all

    def _L1_cond_setup():
        import jax, jax.numpy as jnp
        import numpy as np
        from jax.scipy.linalg import expm
        N, D, COND_DIM = (288, 64, 288)
        B, T = (16, 256)

        def _rotation(cond, W, b):
            v = jax.nn.silu(cond) @ W.T + b
            iu, ju = jnp.triu_indices(D, k=1)
            A = jnp.zeros((cond.shape[0], D, D), dtype=v.dtype)
            A = A.at[:, iu, ju].set(v).at[:, ju, iu].set(-v)
            return expm(A)
        key = jax.random.key(seed)
        k1, k2, k3, k4, k5 = jax.random.split(key, 5)
        x = jax.random.normal(k1, (B, T, N), dtype=jnp.float32)
        cond = jax.random.normal(k2, (B, COND_DIM), dtype=jnp.float32)
        P = jax.random.normal(k3, (N, D), dtype=jnp.float32)
        n_skew = D * (D - 1) // 2
        bound = 1.0 / np.sqrt(COND_DIM)
        W = jax.random.uniform(k4, (n_skew, COND_DIM), minval=-bound, maxval=bound, dtype=jnp.float32)
        b = jax.random.uniform(k5, (n_skew,), minval=-bound, maxval=bound, dtype=jnp.float32)
        return {'x': x, 'cond': cond, 'P': P, 'W': W, 'b': b}
    _L1_cond_all = _L1_cond_setup()
    _L1_cond_in = {k: v for k, v in _L1_cond_all.items() if k in ('P', 'W', 'b')}
    del _L1_cond_all
    return {'x': x, 'cond_1152': cond_1152, 'L0_cond_w_qkv': _L0_cond_in['w_qkv'], 'L0_cond_b_qkv': _L0_cond_in['b_qkv'], 'L0_cond_w_proj': _L0_cond_in['w_proj'], 'L0_cond_b_proj': _L0_cond_in['b_proj'], 'L0_cond_w_fc1': _L0_cond_in['w_fc1'], 'L0_cond_b_fc1': _L0_cond_in['b_fc1'], 'L0_cond_w_fc2': _L0_cond_in['w_fc2'], 'L0_cond_b_fc2': _L0_cond_in['b_fc2'], 'L0_cond_w_ada': _L0_cond_in['w_ada'], 'L0_cond_b_ada': _L0_cond_in['b_ada'], 'L1_cond_P': _L1_cond_in['P'], 'L1_cond_W': _L1_cond_in['W'], 'L1_cond_b': _L1_cond_in['b']}

def reference(x, cond_1152, L0_cond_w_qkv, L0_cond_b_qkv, L0_cond_w_proj, L0_cond_b_proj, L0_cond_w_fc1, L0_cond_b_fc1, L0_cond_w_fc2, L0_cond_b_fc2, L0_cond_w_ada, L0_cond_b_ada, L1_cond_P, L1_cond_W, L1_cond_b):
    import jax
    import jax.numpy as jnp

    def _L0_cond_ref(x, t_emb, w_qkv, b_qkv, w_proj, b_proj, w_fc1, b_fc1, w_fc2, b_fc2, w_ada, b_ada):
        import jax, jax.numpy as jnp
        import numpy as np
        B, N, D = (8, 256, 288)
        H = 16
        HD = D // H
        HID = 4 * D
        EPS = 1e-06

        def _ln(x):
            mu = jnp.mean(x, axis=-1, keepdims=True)
            var = jnp.mean(jnp.square(x - mu), axis=-1, keepdims=True)
            return (x - mu) * jax.lax.rsqrt(var + EPS)

        def _modulate(x, shift, scale):
            return x * (1.0 + scale[:, None, :]) + shift[:, None, :]

        def _attn(x, w_qkv, b_qkv, w_proj, b_proj):
            b, n, d = x.shape
            qkv = (x @ w_qkv + b_qkv).reshape(b, n, 3, H, HD)
            q = qkv[:, :, 0].transpose(0, 2, 1, 3)
            k = qkv[:, :, 1].transpose(0, 2, 1, 3)
            v = qkv[:, :, 2].transpose(0, 2, 1, 3)
            scores = jnp.einsum('bhnd,bhmd->bhnm', q, k) * HD ** (-0.5)
            attn = jax.nn.softmax(scores, axis=-1)
            out = jnp.einsum('bhnm,bhmd->bhnd', attn, v)
            out = out.transpose(0, 2, 1, 3).reshape(b, n, d)
            return out @ w_proj + b_proj
        ada = jax.nn.silu(t_emb) @ w_ada + b_ada
        shift_a, scale_a, gate_a, shift_f, scale_f, gate_f = jnp.split(ada, 6, axis=-1)
        x = x + gate_a[:, None, :] * _attn(_modulate(_ln(x), shift_a, scale_a), w_qkv, b_qkv, w_proj, b_proj)
        h = _modulate(_ln(x), shift_f, scale_f)
        h = jax.nn.gelu(h @ w_fc1 + b_fc1, approximate=True) @ w_fc2 + b_fc2
        return x + gate_f[:, None, :] * h

    def _L1_cond_ref(x, cond, P, W, b):
        import jax, jax.numpy as jnp
        import numpy as np
        from jax.scipy.linalg import expm
        N, D, COND_DIM = (288, 64, 288)
        B, T = (16, 256)

        def _rotation(cond, W, b):
            v = jax.nn.silu(cond) @ W.T + b
            iu, ju = jnp.triu_indices(D, k=1)
            A = jnp.zeros((cond.shape[0], D, D), dtype=v.dtype)
            A = A.at[:, iu, ju].set(v).at[:, ju, iu].set(-v)
            return expm(A)
        U, _ = jnp.linalg.qr(P)
        R = _rotation(cond, W, b)
        z = jnp.einsum('btn,nd->btd', x, U)
        z_rot = jnp.einsum('btd,bde->bte', z, R)
        x_rot = x + jnp.einsum('btd,nd->btn', z_rot - z, U)
        return x_rot
    x = _L0_cond_ref(x, cond_1152, L0_cond_w_qkv, L0_cond_b_qkv, L0_cond_w_proj, L0_cond_b_proj, L0_cond_w_fc1, L0_cond_b_fc1, L0_cond_w_fc2, L0_cond_b_fc2, L0_cond_w_ada, L0_cond_b_ada)
    x = _L1_cond_ref(x, cond_1152, L1_cond_P, L1_cond_W, L1_cond_b)
    return x

_drawn_inputs = setup_inputs


def setup_inputs(seed=0):
    import zlib

    import numpy as np

    out = dict(_drawn_inputs(seed))
    spreads = {}
    factors = {'L0_cond_w_qkv': 8.0,
     'L0_cond_b_qkv': 8.0,
     'L0_cond_w_proj': 8.0,
     'L0_cond_b_proj': 21.529,
     'L0_cond_b_fc1': 60.79,
     'L0_cond_b_fc2': 22.026,
     'L0_cond_b_ada': 8.0,
     'L0_cond_w_fc1': 3.304,
     'L0_cond_w_fc2': 2.947}
    for name, (base, spread) in spreads.items():
        noise = np.random.default_rng([zlib.crc32(name.encode()), seed]).standard_normal(out[name].shape)
        drawn = base * np.exp(spread * noise) if base else spread * noise
        out[name] = jnp.asarray(drawn.astype(out[name].dtype))
    for name, factor in factors.items():
        out[name] = (out[name] * factor).astype(out[name].dtype)
    return out
```

```python
from contextlib import ExitStack

import numpy as np

import concourse.bass as bass
from concourse import mybir

B, N, D = 8, 256, 288
H = 16
HD = D // H
HID = 4 * D
R = 64
P128 = 128
KB, KP = 3, 96
NT = N // P128
FT = HID // P128
HG, GH = 4, 4
HEADS = [6, 5, 5]
STACK = 4 * HD
TAYLOR = 10
SQUARINGS = 19
LN_EPS = 1e-6
KIND = {"shift_a": 0, "scale_a": 1, "gate_a": 2, "shift_f": 3, "scale_f": 4, "gate_f": 5}
MOD = ["shift_a", "scale_a", "shift_f", "scale_f"]
WCHUNK = 8


def at_least(engine, semaphore, value):
    if isinstance(value, int) and value <= 0:
        return
    engine.wait_ge(semaphore, value)


def by_register(engine, semaphore, value, passed):
    engine.wait_ge(semaphore, value)
    engine.sem_inc(passed, 1)


def build(nc, t):
    f32, f32r, i32 = mybir.dt.float32, mybir.dt.float32r, mybir.dt.int32
    ALU, ACT, AX = mybir.AluOpType, mybir.ActivationFunctionType, mybir.AxisListType
    ctx, setup_ctx = ExitStack(), ExitStack()
    with ctx:
        def sb(name, shape, dt=f32, where=ctx):
            return where.enter_context(nc.sbuf_tensor(name, shape, dt))

        def sem(name):
            return ctx.enter_context(nc.semaphore(name))

        ident = sb("ident", [P128, P128])
        sel = sb("sel", [P128, P128])
        x_all = sb("x_all", [P128, B * NT, D])
        wqkv_hi, wqkv_lo = sb("wqkv_hi", [KP, KB, 3 * D], f32r), sb("wqkv_lo", [KP, KB, 3 * D], f32r)
        wfc1_hi, wfc1_lo = sb("wfc1_hi", [KP, KB, HID], f32r), sb("wfc1_lo", [KP, KB, HID], f32r)
        wfc2_hi, wfc2_lo = sb("wfc2_hi", [P128, FT, D], f32r), sb("wfc2_lo", [P128, FT, D], f32r)
        wproj = sb("wproj", [P128, HG, D])
        bqk = sb("bqk", [P128, 6])
        bv = sb("bv", [P128, D])
        bfc1 = sb("bfc1", [P128, FT])
        bfc2 = sb("bfc2", [P128, D])
        mod = sb("mod", [KP, len(MOD) * KB, B])
        U_q = sb("U_q", [KP, KB, R])
        rot_out = sb("rot_out", [R, B, D])
        ones_r = sb("ones_r", [2, N], f32r)
        half = sb("half", [P128, 2])

        def tmp(name, shape, dt=f32):
            return sb(name, shape, dt, setup_ctx)
        wada = tmp("wada", [KP, KB, 6 * D])
        raw_qkv = tmp("raw_qkv", [KP, KB, 3 * D])
        raw_fc1 = tmp("raw_fc1", [KP, KB, HID])
        raw_fc2 = tmp("raw_fc2", [P128, FT, D])
        wskew = tmp("wskew", [KP, 3, KB, WCHUNK, R])
        scond = tmp("scond", [KP, KB, B])
        bada = tmp("bada", [KP, len(MOD) * KB])
        bgate = tmp("bgate", [B, 2 * D])
        gates = tmp("gates", [B, 2 * D])
        bskew = tmp("bskew", [R, R])
        thr = tmp("thr", [R, SQUARINGS])
        striu = tmp("striu", [R, R])
        rowmask = tmp("rowmask", [KP, KB, R])
        ones = tmp("ones", [R, R])
        Pm = tmp("Pm", [KP, KB, R])
        pivot = tmp("pivot", [KP, KB + 1])
        sr = tmp("sr", [KP, 2 * R])
        small = tmp("small", [KP, 16])
        wrow = tmp("wrow", [KP, R])
        Uh = tmp("Uh", [KP, KB, R])
        UhT = tmp("UhT", [R, KB, KP])
        Gm, L, LT, ET, UT1, Xq = (tmp(n, [R, R]) for n in ("Gm", "L", "LT", "ET", "UT1", "Xq"))
        dcol = tmp("dcol", [R, 2])
        QT = tmp("QT", [R, D])
        As, X, XT = (tmp(n, [R, B, R]) for n in ("As", "X", "XT"))
        Ab = tmp("Ab", [R, B, R])
        norm1, scl = tmp("norm1", [R, B]), tmp("scl", [R, B])
        flags = tmp("flags", [R, B, SQUARINGS])
        fi = tmp("fi", [R, SQUARINGS, B], i32)
        keep = tmp("keep", [R, B, R], i32)
        setup_ctx.close()

        xn = sb("xn", [P128, NT, D])
        stats = sb("stats", [P128, NT, 6])
        mv = sb("mv", [P128, 2, NT, 2])
        rstd = sb("rstd", [P128, 2, NT])
        h32 = sb("h32", [KP, KB, N])
        h1_hi, h1_lo = sb("h1_hi", [KP, KB, N], f32r), sb("h1_lo", [KP, KB, N], f32r)
        h2_hi, h2_lo = sb("h2_hi", [KP, KB, N], f32r), sb("h2_lo", [KP, KB, N], f32r)
        NS = 3
        qk_hi, qk_lo = sb("qk_hi", [6 * HD, NS, N], f32r), sb("qk_lo", [6 * HD, NS, N], f32r)
        q_st = sb("q_st", [STACK + 2, H, N], f32r)
        k_st = sb("k_st", [STACK + 2, H, N], f32r)
        v_aug = sb("v_aug", [P128, NT, H, 32])
        probs = sb("probs", [P128, 4, 2, NT, N])
        o_raw = sb("o_raw", [P128, 2, N])
        o_inv = sb("o_inv", [P128, 2, N])
        o_nrm = sb("o_nrm", [P128, HG, N])
        rowmax = sb("rowmax", [P128, NT, H])
        nm_hi, nm_lo = sb("nm_hi", [H, N], f32r), sb("nm_lo", [H, N], f32r)
        gate_bc = sb("gate_bc", [P128, 2 * D])
        gb2 = sb("gb2", [P128, D])
        gated = sb("gated", [P128, 2, D])
        g32 = sb("g32", [P128, NS, N])
        g_hi, g_lo = sb("g_hi", [P128, NS, N], f32r), sb("g_lo", [P128, NS, N], f32r)
        x3 = sb("x3", [P128, NT, D])
        x3T = h32
        z_sb = gated[0:R, 0, 0:N]

        bank = ctx.enter_context(nc.psum_tensor("bank", [P128, 8, 512], f32))

        gate_dram = nc.dram_tensor("gate_scratch", (B, 2 * D), f32).ap()

        names = """consts x_first x_rest wada_in cond_in bias_in p_in qkv_in fc1_in fc2_in
        silu ada_pe gates_pe gates_out gates_stored hi_qkv hi_fc1 hi_fc2 ones_set ones_in pool_set
        wskew_used skew_pe exp_pe exp_dve pivot_out dots_pe dots_out root_out step_out refl_out
        qr_link qr_pe qr_dve link setup_done
        stat1 stat2 mv1 mv2 rstd1 rstd2 xn1 xn2 t1_pe t2_pe h32_1 h32_2 hhi1 hhi2 h1_out h2_out
        qk_pe qk_hi_out qk_lo_out v_pe v_out max_pe max_out maxt_pe nmhi_out nm_out nm_in
        st_pe exp_out pv_pe o_out bc_pe inv_out nrm_out proj_pe gated1 x2_out
        gate_in gb2_out x2b_out fc1_pe gelu_out ghi_out glo_out fc2k_pe gated2 x3_out h32_eps1 h32_eps2 passed passed_pe passed_pool
        t3_pe x3t_out z_pe z_out rot_pe y_out y_stored"""
        S = {n: sem(n) for n in names.split()}
        stack_in = [sem(f"stack_in{i}") for i in range(6)]
        wskew_in = [sem(f"wskew_in{i}") for i in range(3)]
        N_CONSTS = 6

        block = ctx.enter_context(nc.Block())

        @block.sync
        def _(sp):
            def load(dst, src, s):
                sp.dma_start(dst, src).then_inc(s, 16)
            load(scond[:], t["condT"], S["cond_in"])
            load(wada[:], t["w_ada"], S["wada_in"])
            load(bada[:], t["b_ada"], S["wada_in"])
            load(bgate[:], t["b_gate"], S["wada_in"])
            load(ident[:], t["ident"], S["consts"])
            load(sel[:], t["sel"], S["consts"])
            load(striu[:], t["striu"], S["consts"])
            load(rowmask[:], t["rowmask"], S["consts"])
            load(thr[:], t["thr"], S["consts"])
            load(bskew[:], t["b_skew"], S["consts"])
            load(Pm[:], t["P"], S["p_in"])
            load(x_all[:, 0:NT, :], t["x"][0], S["x_first"])
            load(raw_qkv[:], t["w_qkv"], S["qkv_in"])
            for c in range(R // WCHUNK):
                if c >= 3:
                    sp.wait_ge(S["wskew_used"], c - 2)
                load(wskew[:, c % 3], t["w_skew"][:, :, c * WCHUNK:(c + 1) * WCHUNK, :], wskew_in[c % 3])
            load(raw_fc1[:], t["w_fc1"], S["fc1_in"])
            load(raw_fc2[:], t["w_fc2"], S["fc2_in"])
            load(wproj[:], t["w_proj"], S["bias_in"])
            load(bqk[:], t["b_qk"], S["bias_in"])
            load(bfc1[:], t["b_fc1"], S["bias_in"])
            load(bv[:], t["b_v"].partition_broadcast(P128), S["bias_in"])
            load(bfc2[:], t["b_fc2"].partition_broadcast(P128), S["bias_in"])
            for b in range(1, B):
                load(x_all[:, NT * b:NT * (b + 1), :], t["x"][b], S["x_rest"])
            sp.wait_ge(S["gates_out"], 1)
            load(gate_dram, gates[:], S["gates_stored"])
            sp.wait_ge(S["gates_stored"], 16)
            sp.wait_ge(S["ones_set"], 1)
            sp.wait_ge(S["setup_done"], 1)
            load(k_st[STACK:STACK + 2, :, :].bitcast(f32), ones_r[:].bitcast(f32).unsqueeze(1).to_broadcast([2, H, N]), S["ones_in"])
            sp.wait_ge(S["ones_in"], 16)

            def stack(n):
                at_least(sp, S["st_pe"], n * 8)
                for i in range(6):
                    h0, nh = sum(HEADS[:i // 2]), HEADS[i // 2]
                    dst = (q_st, k_st)[i % 2]
                    sp.wait_ge(S["qk_lo_out"], n * 6 + i + 1)
                    for r, low in enumerate(((0, 0, 1, 1), (0, 1, 0, 1))[i % 2]):
                        src = (qk_hi, qk_lo)[low]
                        sp.dma_start(dst[r * HD:(r + 1) * HD, h0:h0 + nh, :].bitcast(f32),
                                     src[0:nh * HD, i % NS, :].bitcast(f32)).then_inc(stack_in[i], 16)

            def negmax(n):
                sp.wait_ge(S["nm_out"], n + 1)
                sp.dma_start(q_st[STACK:STACK + 1, :, :].bitcast(f32), nm_hi[:].bitcast(f32)).then_inc(S["nm_in"], 16)
                sp.dma_start(q_st[STACK + 1:STACK + 2, :, :].bitcast(f32), nm_lo[:].bitcast(f32)).then_inc(S["nm_in"], 16)

            def gate(n):
                at_least(sp, S["x3_out"], n * NT)
                at_least(sp, S["gb2_out"], n)
                sp.dma_start(gate_bc[:], gate_dram[bass.ds(n, 1), :].rearrange("o d -> (o d)")
                             .partition_broadcast(P128)).then_inc(S["gate_in"], 16)

            def store(n):
                sp.wait_ge(S["y_out"], (n + 1) * NT)
                sp.dma_start(t["y"][n], x_all[:, bass.ds(n * NT, NT), :]).then_inc(S["y_stored"], 16)

            stack(0)
            gate(0)
            negmax(0)
            with sp.Fori(0, B - 1) as i:
                stack(i + 1)
                negmax(i + 1)
                gate(i + 1)
                store(i)
            store(B - 1)
            sp.wait_ge(S["y_stored"], 16 * B)

        @block.tensor
        def _(pe):
            def mm(out, lhsT, rhs, start, stop):
                return pe.matmul(out, lhsT, rhs, start=start, stop=stop)

            def mm3(out, lhsT, rhs, start, stop):
                mm(out, lhsT[0], rhs[0], start, False)
                mm(out, lhsT[0], rhs[1], False, False)
                return mm(out, lhsT[1], rhs[0], False, stop)

            pe.wait_ge(S["silu"], 1)
            pe.wait_ge(S["wada_in"], 48)
            for m, name in enumerate(MOD):
                for fb in range(KB):
                    c = KIND[name] * D + fb * KP
                    o = (m * KB + fb) * B
                    for kb in range(KB):
                        last = mm(bank[0:KP, 0, o:o + B], wada[:, kb, c:c + KP], scond[:, kb, :], kb == 0, kb == KB - 1)
            last.then_inc(S["ada_pe"], 1)
            for g, name in enumerate(("gate_a", "gate_f")):
                for kb in range(KB):
                    last = mm(bank[0:B, 1 + g, 0:D], scond[:, kb, :], wada[:, kb, KIND[name] * D:(KIND[name] + 1) * D],
                              kb == 0, kb == KB - 1)
            last.then_inc(S["gates_pe"], 1)
            for c in range(R // WCHUNK):
                pe.wait_ge(wskew_in[c % 3], 16 * (c // 3 + 1))
                for jj in range(WCHUNK):
                    j = c * WCHUNK + jj
                    for kb in range(KB):
                        last = mm(bank[0:R, 3, j:B * R:R], wskew[:, c % 3, kb, jj, :], scond[:, kb, :],
                                  kb == 0, kb == KB - 1)
                last.then_inc(S["wskew_used"], 1)

            exp_dve = [0]

            def after_exp_dve():
                exp_dve[0] += 1
                pe.wait_ge(S["exp_dve"], exp_dve[0])

            def per_sample(bk, lhsT, rhs):
                for b in range(B):
                    last = mm(bank[0:R, bk, b * R:(b + 1) * R], lhsT[:, b, :], rhs[:, b, :], True, True)
                return last

            def transposes(bk, src):
                for b in range(B):
                    last = pe.transpose(bank[0:R, bk, b * R:(b + 1) * R], src[:, b, :], ident[0:R, 0:R])
                return last

            pe.wait_ge(S["consts"], 16 * N_CONSTS)
            after_exp_dve()
            transposes(4, Ab).then_inc(S["exp_pe"], 1)
            after_exp_dve()
            pe.wait_ge(S["pool_set"], 1)
            mm(bank[0:R, 5, :], ones[:], X[:].rearrange("p b j -> p (b j)"), True, True).then_inc(S["exp_pe"], 1)
            for k in range(TAYLOR - 1, 0, -1):
                after_exp_dve()
                per_sample(5, As, X).then_inc(S["exp_pe"], 1)
            after_exp_dve()
            transposes(4, X).then_inc(S["exp_pe"], 1)
            e0 = exp_dve[0]
            with pe.Fori(0, SQUARINGS) as k:
                by_register(pe, S["exp_dve"], k + (e0 + 1), S["passed_pe"])
                per_sample(5, XT, X)
                per_sample(6, X, XT).then_inc(S["exp_pe"], 1)

            pe.wait_ge(S["p_in"], 16)
            with pe.Fori(0, R) as j:
                pe.wait_ge(S["pivot_out"], j + 1)
                for kb in range(KB):
                    mm(bank[0:KP, 0, 0:R], pivot[:, kb:kb + 1].to_broadcast([KP, KP]), Pm[:, kb, :], kb == 0, kb == KB - 1)
                mm(bank[0:KP, 0, R:2 * R], pivot[:, KB:KB + 1].to_broadcast([KP, KP]), Pm[:, 0, :],
                   True, True).then_inc(S["dots_pe"], 1)

            qr_dve = [0]

            def after_qr_dve():
                qr_dve[0] += 1
                pe.wait_ge(S["qr_dve"], qr_dve[0])

            after_qr_dve()
            for kb in range(KB):
                mm(bank[0:R, 0, 0:R], Uh[:, kb, :], Uh[:, kb, :], kb == 0, kb == KB - 1)
            for kb in range(KB):
                last = pe.transpose(bank[0:R, 1, kb * KP:(kb + 1) * KP], Uh[:, kb, :], ident[0:KP, 0:KP])
            last.then_inc(S["qr_pe"], 1)
            after_qr_dve()
            pe.transpose(bank[0:R, 2, 0:R], L[:], ident[0:R, 0:R]).then_inc(S["qr_pe"], 1)
            for k in range(5):
                after_qr_dve()
                mm(bank[0:R, 3, 0:R], LT[:], L[:], True, True)
                mm(bank[0:R, 4, 0:R], L[:], LT[:], True, True).then_inc(S["qr_pe"], 1)
                after_qr_dve()
                mm(bank[0:R, 5, 0:R], L[:], ET[:], True, True).then_inc(S["qr_pe"], 1)
            after_qr_dve()
            mm(bank[0:R, 5, 0:R], ET[:], UT1[:], True, True).then_inc(S["qr_pe"], 1)
            after_qr_dve()
            for kb in range(KB):
                mm(bank[0:KP, 6, kb * R:(kb + 1) * R], UhT[:, kb, :], Xq[:], True, True)
            mm(bank[0:R, 7, 0:D], Xq[:], UhT[:].rearrange("p a b -> p (a b)"), True, True).then_inc(S["qr_pe"], 1)
            after_qr_dve()
            for b in range(B):
                at_least(pe, S["qr_dve"], qr_dve[0] + b - 1 if b >= 2 else 0)
                mm(bank[0:R, b % 2, 0:D], XT[:, b, :], QT[:], True, True).then_inc(S["qr_pe"], 1)

            def transpose_rows(bk, src, done):
                for kb in range(KB):
                    for tt in range(NT):
                        o = kb % 2 * N + tt * P128
                        last = pe.transpose(bank[0:KP, bk + kb // 2, o:o + P128], src[:, tt, kb * KP:(kb + 1) * KP],
                                            ident[:])
                last.then_inc(done, 1)

            def t1(n):
                pe.wait_ge(S["xn1"], (n + 1) * NT)
                transpose_rows(0, xn, S["t1_pe"])

            def qk(n):
                pe.wait_ge(S["h1_out"], (n + 1) * KB)
                for i in range(6):
                    h0, nh = sum(HEADS[:i // 2]), HEADS[i // 2]
                    c = i % 2 * D + h0 * HD
                    if i >= 4:
                        pe.wait_ge(S["qk_lo_out"], n * 6 + i - 3)
                    for kb in range(KB):
                        last = mm3(bank[0:nh * HD, 2 + i % 4, 0:N],
                                   (wqkv_hi[:, kb, c:c + nh * HD], wqkv_lo[:, kb, c:c + nh * HD]),
                                   (h1_hi[:, kb, :], h1_lo[:, kb, :]), kb == 0, kb == KB - 1)
                    last.then_inc(S["qk_pe"], 1)

            def v(n):
                for tt in range(NT):
                    for kb in range(KB):
                        last = mm3(bank[:, tt, 0:D], (h1_hi[:, kb, tt * P128:(tt + 1) * P128],
                                                      h1_lo[:, kb, tt * P128:(tt + 1) * P128]),
                                   (wqkv_hi[:, kb, 2 * D:3 * D], wqkv_lo[:, kb, 2 * D:3 * D]), kb == 0, kb == KB - 1)
                    last.then_inc(S["v_pe"], 1)

            def max_scores(n, h):
                i = 0 if h < HEADS[0] else (1 if h < HEADS[0] + HEADS[1] else 2)
                if h in (0, HEADS[0], HEADS[0] + HEADS[1]):
                    pe.wait_ge(stack_in[2 * i], (n + 1) * 64)
                    pe.wait_ge(stack_in[2 * i + 1], (n + 1) * 64)
                if h == 0:
                    pe.wait_ge(S["qk_lo_out"], n * 6 + 4)
                if h >= 2:
                    pe.wait_ge(S["max_out"], n * H + h - 1)
                for tt in range(NT):
                    last = mm(bank[:, 4 + h % 2, tt * N:(tt + 1) * N], q_st[0:STACK, h, tt * P128:(tt + 1) * P128],
                              k_st[0:STACK, h, :], True, True)
                last.then_inc(S["max_pe"], 1)

            def max_transpose(n):
                pe.wait_ge(S["max_out"], (n + 1) * H)
                for tt in range(NT):
                    last = pe.transpose(bank[0:H, 7, tt * P128:(tt + 1) * P128], rowmax[:, tt, :], ident[:])
                last.then_inc(S["maxt_pe"], 1)

            def scores(n, i):
                if i == 0:
                    pe.wait_ge(S["nm_in"], (n + 1) * 32)
                    pe.wait_ge(S["ones_in"], 16)
                if i >= 2:
                    pe.wait_ge(S["exp_out"], n * 8 + i - 1)
                for hh in range(2):
                    for tt in range(NT):
                        last = mm(bank[:, 2 + i % 2 * 2 + hh, tt * N:(tt + 1) * N],
                                  k_st[:, 2 * i + hh, tt * P128:(tt + 1) * P128], q_st[:, 2 * i + hh, :], True, True)
                last.then_inc(S["st_pe"], 1)

            def pv(n, g):
                pe.wait_ge(S["exp_out"], n * 8 + 2 * g + 2)
                if g == 0:
                    pe.wait_ge(S["v_out"], (n + 1) * NT)
                    pe.wait_ge(S["nm_out"], n + 1)
                else:
                    at_least(pe, S["nrm_out"], n * HG + g - 1)
                for tt in range(NT):
                    for j in range(GH):
                        h = GH * g + j
                        last = mm(bank[32 * j:32 * j + 32, 6 + g % 2, 0:N], v_aug[:, tt, h, :],
                                  probs[:, h // 2 % 4, h % 2, tt, :], tt == 0, tt == NT - 1)
                last.then_inc(S["pv_pe"], 1)

            def sums(n, g):
                pe.wait_ge(S["o_out"], n * HG + g + 1)
                mm(bank[:, 6 + g % 2, N:2 * N], sel[:], o_raw[:, g % 2, :], True, True).then_inc(S["bc_pe"], 1)

            def proj(n):
                pe.wait_ge(S["nrm_out"], (n + 1) * HG)
                for tt in range(NT):
                    for g in range(HG):
                        last = mm(bank[:, tt, 0:D], o_nrm[:, g, tt * P128:(tt + 1) * P128], wproj[:, g, :],
                                  g == 0, g == HG - 1)
                    last.then_inc(S["proj_pe"], 1)

            def t2(n):
                pe.wait_ge(S["xn2"], (n + 1) * NT)
                transpose_rows(6, xn, S["t2_pe"])

            FC1_BANK = (2, 3, 6)

            def fc1(n, j):
                if j == 0:
                    pe.wait_ge(S["h2_out"], (n + 1) * KB)
                if j >= 3:
                    pe.wait_ge(S["gelu_out"], n * FT + j - 2)
                for kb in range(KB):
                    last = mm3(bank[:, FC1_BANK[j % 3], 0:N],
                               (wfc1_hi[:, kb, j * P128:(j + 1) * P128], wfc1_lo[:, kb, j * P128:(j + 1) * P128]),
                               (h2_hi[:, kb, :], h2_lo[:, kb, :]), kb == 0, kb == KB - 1)
                last.then_inc(S["fc1_pe"], 1)

            def fc2(n, k):
                pe.wait_ge(S["glo_out"], n * FT + k + 1)
                if k == 0:
                    pe.wait_ge(S["x2_out"], (n + 1) * NT)
                for tt in range(NT):
                    last = mm3(bank[:, tt, 0:D], (g_hi[:, k % NS, tt * P128:(tt + 1) * P128],
                                                  g_lo[:, k % NS, tt * P128:(tt + 1) * P128]),
                               (wfc2_hi[:, k, :], wfc2_lo[:, k, :]), k == 0, k == FT - 1)
                last.then_inc(S["fc2k_pe"], 1)

            def mlp(n, following):
                if following is not None:
                    pe.wait_ge(S["v_out"], (following + 1) * NT)
                for j in range(FT):
                    fc1(n, j)
                    if j >= 2:
                        fc2(n, j - 2)
                    if following is not None and j >= 1:
                        max_scores(following, 2 * j - 2)
                        max_scores(following, 2 * j - 1)
                if following is not None:
                    max_transpose(following)
                for k in range(FT - 2, FT):
                    fc2(n, k)

            def rot_transpose(n):
                pe.wait_ge(S["x3_out"], (n + 1) * NT)
                transpose_rows(0, x3, S["t3_pe"])

            def rot_z(n):
                pe.wait_ge(S["x3t_out"], n + 1)
                for kb in range(KB):
                    last = mm(bank[0:R, 0, 0:N], U_q[:, kb, :], x3T[:, kb, :], kb == 0, kb == KB - 1)
                last.then_inc(S["z_pe"], 1)

            def rot_back(n):
                pe.wait_ge(S["z_out"], n + 1)
                for tt in range(NT):
                    mm(bank[:, tt, 0:D], gated[0:R, 0, tt * P128:(tt + 1) * P128],
                       rot_out[:, bass.ds(n, 1), :].rearrange("p o d -> p (o d)"), True, True).then_inc(S["rot_pe"], 1)

            def attention(n, previous, following):
                scores(n, 0)
                scores(n, 1)
                if previous is not None:
                    rot_transpose(previous)
                scores(n, 2)
                scores(n, 3)
                pv(n, 0)
                if previous is not None:
                    rot_z(previous)
                scores(n, 4)
                scores(n, 5)
                pv(n, 1)
                if previous is not None:
                    rot_back(previous)
                sums(n, 0)
                scores(n, 6)
                scores(n, 7)
                if following is not None:
                    if previous is not None:
                        pe.wait_ge(S["y_out"], (previous + 1) * NT)
                    t1(following)
                pv(n, 2)
                sums(n, 1)
                pv(n, 3)
                sums(n, 2)
                sums(n, 3)

            def step(i, last_attention):
                if not last_attention:
                    pe.wait_ge(S["h32_1"], (i + 2) * KB)
                else:
                    pe.wait_ge(S["h32_1"], B * KB)
                proj(i)
                qk(i + 1)
                t2(i)
                pe.wait_ge(S["x2_out"], (i + 1) * NT)
                v(i + 1)
                mlp(i, i + 1)
                attention(i + 1, i, None if last_attention else i + 2)

            pe.wait_ge(S["setup_done"], 1)
            t1(0)
            pe.wait_ge(S["h1_out"], KB)
            qk(0)
            v(0)
            for h in range(H):
                max_scores(0, h)
            max_transpose(0)
            attention(0, None, 1)
            with pe.Fori(0, B - 2) as i:
                step(i, False)
            step(B - 2, True)
            pe.wait_ge(S["y_out"], (B - 1) * NT)
            proj(B - 1)
            t2(B - 1)
            mlp(B - 1, None)
            rot_transpose(B - 1)
            rot_z(B - 1)
            rot_back(B - 1)

        @block.scalar
        def _(act):
            act.wait_ge(S["cond_in"], 16)
            act.activation(scond[:], scond[:], ACT.Silu).then_inc(S["silu"], 1)
            for raw, hi, arrived, done in ((raw_qkv, wqkv_hi, "qkv_in", "hi_qkv"), (raw_fc1, wfc1_hi, "fc1_in", "hi_fc1"),
                                           (raw_fc2, wfc2_hi, "fc2_in", "hi_fc2")):
                act.wait_ge(S[arrived], 16)
                act.activation(hi[:], raw[:], ACT.Copy).then_inc(S[done], 1)
            act.wait_ge(S["bias_in"], 16 * 5)
            act.wait_ge(S["setup_done"], 1)

            def qk(n):
                for i in range(6):
                    nh = HEADS[i // 2]
                    act.wait_ge(S["qk_pe"], n * 6 + i + 1)
                    k = (i - NS) % 6
                    at_least(act, stack_in[k], (n if i < NS else n + 1) * 64)
                    act.activation(qk_hi[0:nh * HD, i % NS, :], bank[0:nh * HD, 2 + i % 4, 0:N], ACT.Identity,
                                   bias=bqk[0:nh * HD, i:i + 1]).then_inc(S["qk_hi_out"], 1)

            def h2(n):
                for kb in range(KB):
                    act.wait_ge(S["h32_2"], n * KB + kb + 1)
                    act.activation(h2_hi[:, kb, :], h32[:, kb, :], ACT.Copy).then_inc(S["hhi2"], 1)

            def exp(n, i):
                act.wait_ge(S["st_pe"], n * 8 + i + 1)
                at_least(act, S["pv_pe"], n * HG + i // 2 - 1 if i >= 4 else n * HG)
                act.activation(probs[:, i % 4].rearrange("p h t n -> p (h t n)"),
                               bank[:, 2 + i % 2 * 2:4 + i % 2 * 2, :].rearrange("p h n -> p (h n)"),
                               ACT.Exp, scale=float(HD) ** -0.5).then_inc(S["exp_out"], 1)

            def o_copy(n, g):
                act.wait_ge(S["pv_pe"], n * HG + g + 1)
                at_least(act, S["nrm_out"], n * HG + g - 1 if g >= 1 else n * HG)
                act.activation(o_raw[:, g % 2, :], bank[:, 6 + g % 2, 0:N], ACT.Copy).then_inc(S["o_out"], 1)

            def attention(n):
                exp(n, 0)
                exp(n, 1)
                exp(n, 2)
                exp(n, 3)
                o_copy(n, 0)
                exp(n, 4)
                exp(n, 5)
                o_copy(n, 1)
                exp(n, 6)
                exp(n, 7)
                o_copy(n, 2)
                o_copy(n, 3)

            def gelu(n):
                for j in range(FT):
                    act.wait_ge(S["fc1_pe"], n * FT + j + 1)
                    if j >= NS:
                        act.wait_ge(S["fc2k_pe"], n * FT + j - 2)
                    act.activation(g32[:, j % NS, :], bank[:, (2, 3, 6)[j % 3], 0:N], ACT.Gelu_apprx_tanh,
                                   bias=bfc1[:, j:j + 1]).then_inc(S["gelu_out"], 1)
                    act.wait_ge(S["gelu_out"], n * FT + j + 1)
                    act.activation(g_hi[:, j % NS, :], g32[:, j % NS, :], ACT.Copy).then_inc(S["ghi_out"], 1)

            def step(i):
                qk(i + 1)
                h2(i)
                gelu(i)
                attention(i + 1)

            qk(0)
            attention(0)
            with act.Fori(0, B - 1) as i:
                step(i)
            h2(B - 1)
            gelu(B - 1)

        @block.gpsimd
        def _(pool):
            pool.memset(ones[:], 1.0)
            pool.memset(half[:, 0:1], -0.5)
            pool.memset(half[:, 1:2], 0.5).then_inc(S["pool_set"], 1)
            pool.wait_ge(S["pool_set"], 1)
            with pool.Fori(0, R) as j:
                pool.wait_ge(S["dots_out"], j + 1)
                pool.tensor_tensor(small[:, 0:1], small[:, 7:8], half[0:KP, 1:2], ALU.pow).then_inc(S["root_out"], 1)
            pool.wait_ge(S["setup_done"], 1)

            def rstd_of(w, n, mv_sem, eps_sem, out_sem):
                by_register(pool, mv_sem, (n + 1) * NT, S["passed_pool"])
                pool.tensor_scalar(rstd[:, w, :], mv[:, w, :, 1], LN_EPS, None, ALU.add).then_inc(eps_sem, 1)
                pool.wait_ge(eps_sem, n + 1)
                pool.tensor_tensor(rstd[:, w, :], rstd[:, w, :], half[:, 0:1].to_broadcast([P128, NT]),
                                   ALU.pow).then_inc(out_sem, 1)

            def x2_bias(n):
                pool.wait_ge(S["gate_in"], (n + 1) * 16)
                pool.tensor_tensor(gb2[:], gate_bc[:, D:2 * D], bfc2[:], ALU.mult).then_inc(S["gb2_out"], 1)
                pool.wait_ge(S["gb2_out"], n + 1)
                pool.wait_ge(S["xn2"], (n + 1) * NT)
                x2 = x_all[:, bass.ds(n * NT, NT), :]
                pool.tensor_tensor(x2, x2, gb2[:].unsqueeze(1).to_broadcast([P128, NT, D]), ALU.add).then_inc(S["x2b_out"], 1)

            def g_low(n):
                for j in range(FT):
                    pool.wait_ge(S["ghi_out"], n * FT + j + 1)
                    pool.tensor_tensor(g_lo[:, j % NS, :], g32[:, j % NS, :], g_hi[:, j % NS, :].bitcast(f32),
                                       ALU.subtract).then_inc(S["glo_out"], 1)

            rstd_of(0, 0, S["mv1"], S["h32_eps1"], S["rstd1"])
            rstd_of(0, 1, S["mv1"], S["h32_eps1"], S["rstd1"])

            def step(i, last_attention):
                rstd_of(1, i, S["mv2"], S["h32_eps2"], S["rstd2"])
                x2_bias(i)
                g_low(i)
                if not last_attention:
                    rstd_of(0, i + 2, S["mv1"], S["h32_eps1"], S["rstd1"])

            with pool.Fori(0, B - 2) as i:
                step(i, False)
            step(B - 2, True)
            step(B - 1, True)

        @block.vector
        def _(dve):
            links = [0]

            def link(ins):
                links[0] += 1
                ins.then_inc(S["link"], 1)
                dve.wait_ge(S["link"], links[0])

            dve.memset(ones_r[:].bitcast(f32), 1.0).then_inc(S["ones_set"], 1)
            dve.wait_ge(S["wada_in"], 48)
            dve.wait_ge(S["ada_pe"], 1)
            link(dve.tensor_tensor(mod[:], bank[0:KP, 0, 0:len(MOD) * KB * B].rearrange("p (m b) -> p m b", b=B),
                                   bada[:].unsqueeze(2).to_broadcast([KP, len(MOD) * KB, B]), ALU.add))
            for m in (1, 3):
                link(dve.tensor_scalar(mod[:, m * KB:(m + 1) * KB, :], mod[:, m * KB:(m + 1) * KB, :], 1.0, None, ALU.add))
            dve.wait_ge(S["gates_pe"], 1)
            dve.tensor_tensor(gates[:].rearrange("p (g d) -> p g d", g=2), bank[0:B, 1:3, 0:D],
                              bgate[:].rearrange("p (g d) -> p g d", g=2), ALU.add).then_inc(S["gates_out"], 1)
            for raw, hi, lo, done in ((raw_qkv, wqkv_hi, wqkv_lo, "hi_qkv"), (raw_fc1, wfc1_hi, wfc1_lo, "hi_fc1"),
                                      (raw_fc2, wfc2_hi, wfc2_lo, "hi_fc2")):
                dve.wait_ge(S[done], 1)
                dve.tensor_tensor(lo[:], raw[:], hi[:].bitcast(f32), ALU.subtract)

            dve.wait_ge(S["consts"], 16 * N_CONSTS)
            exp_pe = [0]

            def after_exp_pe():
                exp_pe[0] += 1
                dve.wait_ge(S["exp_pe"], exp_pe[0])

            def samples(bk):
                return bank[0:R, bk, :].rearrange("p (b j) -> p b j", j=R)

            eye = ident[0:R, 0:R].unsqueeze(1).to_broadcast([R, B, R])
            dve.wait_ge(S["wskew_used"], R // WCHUNK)
            dve.tensor_tensor(Ab[:], samples(3), bskew[:].unsqueeze(1).to_broadcast([R, B, R]),
                              ALU.add).then_inc(S["exp_dve"], 1)
            dve.wait_ge(S["exp_dve"], 1)
            after_exp_pe()
            link(dve.tensor_tensor(As[:], Ab[:], samples(4), ALU.subtract))
            dve.scalar_tensor_tensor(X[:], As[:], -1.0, As[:], ALU.mult, ALU.max).then_inc(S["exp_dve"], 1)
            after_exp_pe()
            link(dve.tensor_reduce(norm1[:], samples(5), AX.X, ALU.max))
            link(dve.tensor_tensor(flags[:], norm1[:].unsqueeze(2).to_broadcast([R, B, SQUARINGS]),
                                   thr[:].unsqueeze(1).to_broadcast([R, B, SQUARINGS]), ALU.is_gt))
            link(dve.tensor_copy(fi[:], flags[:].rearrange("p b k -> p k b")))
            link(dve.tensor_tensor(flags[:], flags[:], thr[:].unsqueeze(1).to_broadcast([R, B, SQUARINGS]), ALU.mult))
            link(dve.tensor_reduce(scl[:], flags[:], AX.X, ALU.add))
            link(dve.tensor_scalar(scl[:], scl[:], 1.0, None, ALU.add))
            link(dve.reciprocal(scl[:], scl[:]))
            link(dve.tensor_tensor(As[:], As[:], scl[:].unsqueeze(2).to_broadcast([R, B, R]), ALU.mult))
            dve.scalar_tensor_tensor(X[:], As[:], 1.0 / TAYLOR, eye, ALU.mult, ALU.add).then_inc(S["exp_dve"], 1)
            for k in range(TAYLOR - 1, 0, -1):
                after_exp_pe()
                dve.scalar_tensor_tensor(X[:], samples(5), -1.0 / k, eye, ALU.mult, ALU.add).then_inc(S["exp_dve"], 1)
            after_exp_pe()
            dve.tensor_copy(XT[:], samples(4)).then_inc(S["exp_dve"], 1)
            e0 = exp_pe[0]
            d0 = 2 + 1 + (TAYLOR - 1) + 1
            with dve.Fori(0, SQUARINGS) as k:
                dve.wait_ge(S["exp_dve"], k + d0)
                dve.tensor_copy(keep[:], fi[:, bass.ds(k, 1), :].rearrange("p o b -> p (o b)").unsqueeze(2)
                                .to_broadcast([R, B, R])).then_inc(S["step_out"], 1)
                dve.wait_ge(S["step_out"], k + 1)
                by_register(dve, S["exp_pe"], k + (e0 + 1), S["passed"])
                dve.copy_predicated(X[:], keep[:], samples(5))
                dve.copy_predicated(XT[:], keep[:], samples(6)).then_inc(S["exp_dve"], 1)
            dve.wait_ge(S["exp_dve"], d0 + SQUARINGS)
            link(dve.tensor_tensor(XT[:], XT[:], eye, ALU.subtract))

            dve.wait_ge(S["p_in"], 16)
            LINKS = 7
            with dve.Fori(0, R) as j:
                at = [0]

                def qlink(ins):
                    at[0] += 1
                    ins.then_inc(S["qr_link"], 1)
                    dve.wait_ge(S["qr_link"], j * LINKS + at[0])

                jcol = bass.ds(j, 1)
                alpha, gb, den, inv, hs, dot = (small[:, c:c + 1] for c in (1, 2, 3, 4, 5, 7))
                dve.tensor_tensor(pivot[:, 0:KB], Pm[:, :, jcol].rearrange("p a o -> p (a o)"),
                                  rowmask[:, :, jcol].rearrange("p a o -> p (a o)"), ALU.mult)
                dve.tensor_copy(pivot[:, KB:KB + 1], ident[0:KP, jcol]).then_inc(S["pivot_out"], 1)
                dve.wait_ge(S["dots_pe"], j + 1)
                qlink(dve.tensor_copy(sr[:], bank[0:KP, 0, 0:2 * R]))
                dve.tensor_copy(dot, sr[:, jcol]).then_inc(S["dots_out"], 1)
                qlink(dve.tensor_copy(alpha, sr[:, bass.ds(j + R, 1)]))
                qlink(dve.tensor_scalar(hs, alpha, 0.0, 0.5, ALU.is_ge, ALU.subtract))
                dve.wait_ge(S["root_out"], j + 1)
                qlink(dve.scalar_tensor_tensor(gb, hs, 2.0, small[:, 0:1], ALU.mult, ALU.mult))
                dve.scalar_tensor_tensor(wrow[:], sr[:, R:2 * R], gb, sr[:, 0:R], ALU.mult, ALU.add)
                qlink(dve.scalar_tensor_tensor(den, alpha, gb, dot, ALU.mult, ALU.add))
                dve.scalar_tensor_tensor(pivot[:, 0:1], pivot[:, KB:KB + 1], gb, pivot[:, 0:1], ALU.mult, ALU.add)
                qlink(dve.reciprocal(inv, den))
                qlink(dve.tensor_scalar(small[:, 8:8 + KB], pivot[:, 0:KB], inv, -1.0, ALU.mult, ALU.mult))
                dve.tensor_copy(Uh[:, :, jcol].rearrange("p a o -> p (a o)"), pivot[:, 0:KB])
                for kb in range(KB):
                    last = dve.scalar_tensor_tensor(Pm[:, kb, :], wrow[:], small[:, 8 + kb:9 + kb], Pm[:, kb, :],
                                                    ALU.mult, ALU.add)
                last.then_inc(S["refl_out"], 1)
                dve.wait_ge(S["refl_out"], j + 1)
                assert at[0] == LINKS

            qr_pe = [0]

            def after_qr_pe():
                qr_pe[0] += 1
                dve.wait_ge(S["qr_pe"], qr_pe[0])

            eye1 = ident[0:R, 0:R]
            dve.tensor_copy(small[0:1, 15:16], small[0:1, 0:1]).then_inc(S["qr_dve"], 1)
            after_qr_pe()
            dve.tensor_copy(Gm[:], bank[0:R, 0, 0:R])
            link(dve.tensor_copy(UhT[:].rearrange("p a b -> p (a b)"), bank[0:R, 1, 0:D]))
            link(dve.tensor_tensor(Xq[:], Gm[:], eye1, ALU.mult))
            link(dve.tensor_reduce(dcol[:, 0:1], Xq[:], AX.X, ALU.add))
            link(dve.tensor_scalar(dcol[:, 0:1], dcol[:, 0:1], 0.5, None, ALU.mult))
            link(dve.reciprocal(dcol[:, 1:2], dcol[:, 0:1]))
            link(dve.tensor_tensor(Gm[:], Gm[:], striu[:], ALU.mult))
            dve.tensor_scalar(UT1[:], UhT[:, 0, 0:R], dcol[:, 1:2], None, ALU.mult)
            dve.tensor_scalar(L[:], Gm[:], dcol[:, 1:2], -1.0, ALU.mult, ALU.mult).then_inc(S["qr_dve"], 1)
            after_qr_pe()
            link(dve.tensor_copy(LT[:], bank[0:R, 2, 0:R]))
            dve.tensor_tensor(ET[:], LT[:], eye1, ALU.add).then_inc(S["qr_dve"], 1)
            for k in range(5):
                after_qr_pe()
                dve.tensor_copy(L[:], bank[0:R, 3, 0:R])
                dve.tensor_copy(LT[:], bank[0:R, 4, 0:R]).then_inc(S["qr_dve"], 1)
                after_qr_pe()
                dve.tensor_tensor(ET[:], ET[:], bank[0:R, 5, 0:R], ALU.add).then_inc(S["qr_dve"], 1)
            after_qr_pe()
            dve.tensor_scalar(Xq[:], bank[0:R, 5, 0:R], -1.0, None, ALU.mult).then_inc(S["qr_dve"], 1)
            after_qr_pe()
            dve.tensor_copy(U_q[:], bank[0:KP, 6, 0:KB * R].rearrange("p (a j) -> p a j", a=KB))
            link(dve.tensor_copy(QT[:], bank[0:R, 7, 0:D]))
            link(dve.tensor_tensor(U_q[:, 0, :], U_q[:, 0, :], ident[0:KP, 0:R], ALU.add))
            dve.tensor_tensor(QT[:, 0:R], QT[:, 0:R], eye1, ALU.add).then_inc(S["qr_dve"], 1)
            for b in range(B):
                after_qr_pe()
                last = dve.tensor_copy(rot_out[:, b, :], bank[0:R, b % 2, 0:D]).then_inc(S["qr_dve"], 1)
            dve.wait_ge(S["pool_set"], 1)
            dve.memset(v_aug[:], 1.0).then_inc(S["setup_done"], 1)
            dve.wait_ge(S["setup_done"], 1)
            dve.wait_ge(S["bias_in"], 16 * 5)

            def xt(n, tt):
                return x_all[:, bass.ds(n * NT + tt, 1), :].rearrange("p o d -> p (o d)")

            def norm_stats(n, w, stat_sem, mv_sem):
                for tt in range(NT):
                    if w == 1:
                        by_register(dve, S["x2_out"], n * NT + tt + 1, S["passed"])
                    dve.bn_stats(stats[:, tt, :], xt(n, tt)).then_inc(stat_sem, 1)
                for tt in range(NT):
                    by_register(dve, stat_sem, n * NT + tt + 1, S["passed"])
                    dve.bn_aggr(mv[:, w, tt, :], stats[:, tt, :]).then_inc(mv_sem, 1)

            def norm_apply(n, w, rstd_sem, out_sem):
                dve.wait_ge(rstd_sem, n + 1)
                for tt in range(NT):
                    dve.tensor_scalar(xn[:, tt, :], xt(n, tt), mv[:, w, tt, 0:1], rstd[:, w, tt:tt + 1],
                                      ALU.subtract, ALU.mult).then_inc(out_sem, 1)

            def h32_of(n, kb, bk, m, out_sem):
                col = bass.ds(n, 1)
                dve.tensor_scalar(h32[:, kb, :], bank[0:KP, bk + kb // 2, kb % 2 * N:kb % 2 * N + N],
                                  mod[:, (m + 1) * KB + kb, col], mod[:, m * KB + kb, col],
                                  ALU.mult, ALU.add).then_inc(out_sem, 1)

            def h1(n):
                dve.wait_ge(S["t1_pe"], n + 1)
                for kb in range(KB):
                    h32_of(n, kb, 0, 0, S["h32_1"])
                for kb in range(KB):
                    dve.wait_ge(S["h32_1"], n * KB + kb + 1)
                    dve.tensor_copy(h1_hi[:, kb, :], h32[:, kb, :]).then_inc(S["hhi1"], 1)
                for kb in range(KB):
                    dve.wait_ge(S["hhi1"], n * KB + kb + 1)
                    dve.tensor_tensor(h1_lo[:, kb, :], h32[:, kb, :], h1_hi[:, kb, :].bitcast(f32),
                                      ALU.subtract).then_inc(S["h1_out"], 1)

            def h2(n):
                dve.wait_ge(S["t2_pe"], n + 1)
                for kb in range(KB):
                    h32_of(n, kb, 6, 2, S["h32_2"])
                for kb in range(KB):
                    dve.wait_ge(S["hhi2"], n * KB + kb + 1)
                    dve.tensor_tensor(h2_lo[:, kb, :], h32[:, kb, :], h2_hi[:, kb, :].bitcast(f32),
                                      ALU.subtract).then_inc(S["h2_out"], 1)

            def qk_low(n, i):
                nh = HEADS[i // 2]
                dve.wait_ge(S["qk_hi_out"], n * 6 + i + 1)
                dve.scalar_tensor_tensor(qk_lo[0:nh * HD, i % NS, :], bank[0:nh * HD, 2 + i % 4, 0:N],
                                         bqk[0:nh * HD, i:i + 1], qk_hi[0:nh * HD, i % NS, :].bitcast(f32),
                                         ALU.add, ALU.subtract).then_inc(S["qk_lo_out"], 1)

            def v_out(n):
                for tt in range(NT):
                    dve.wait_ge(S["v_pe"], n * NT + tt + 1)
                    dve.tensor_tensor(v_aug[:, tt, :, 0:HD], bank[:, tt, 0:D].rearrange("p (h d) -> p h d", d=HD),
                                      bv[:].rearrange("p (h d) -> p h d", d=HD), ALU.add).then_inc(S["v_out"], 1)

            def row_max(n, h):
                dve.wait_ge(S["max_pe"], n * H + h + 1)
                dve.tensor_reduce(rowmax[:, :, h], bank[:, 4 + h % 2, :].rearrange("p (t m) -> p t m", t=NT),
                                  AX.X, ALU.max).then_inc(S["max_out"], 1)

            def neg_max(n):
                dve.wait_ge(S["maxt_pe"], n + 1)
                at_least(dve, S["nm_in"], n * 32)
                dve.tensor_scalar(nm_hi[:], bank[0:H, 7, 0:N], -1.0, None, ALU.mult).then_inc(S["nmhi_out"], 1)
                dve.wait_ge(S["nmhi_out"], n + 1)
                dve.scalar_tensor_tensor(nm_lo[:], bank[0:H, 7, 0:N], -1.0, nm_hi[:].bitcast(f32), ALU.mult,
                                         ALU.subtract).then_inc(S["nm_out"], 1)

            def normalize(n, g):
                dve.wait_ge(S["bc_pe"], n * HG + g + 1)
                dve.reciprocal(o_inv[:, g % 2, :], bank[:, 6 + g % 2, N:2 * N]).then_inc(S["inv_out"], 1)
                dve.wait_ge(S["inv_out"], n * HG + g + 1)
                dve.tensor_tensor(o_nrm[:, g, :], o_raw[:, g % 2, :], o_inv[:, g % 2, :],
                                  ALU.mult).then_inc(S["nrm_out"], 1)

            def x2(n):
                dve.wait_ge(S["gate_in"], (n + 1) * 16)
                for tt in range(NT):
                    dve.wait_ge(S["proj_pe"], n * NT + tt + 1)
                    dve.tensor_tensor(gated[:, tt, :], bank[:, tt, 0:D], gate_bc[:, 0:D], ALU.mult).then_inc(S["gated1"], 1)
                for tt in range(NT):
                    dve.wait_ge(S["gated1"], n * NT + tt + 1)
                    dve.tensor_tensor(xt(n, tt), xt(n, tt), gated[:, tt, :], ALU.add).then_inc(S["x2_out"], 1)

            def x3_out(n):
                dve.wait_ge(S["fc2k_pe"], (n + 1) * FT)
                dve.wait_ge(S["x2b_out"], n + 1)
                for tt in range(NT):
                    dve.tensor_tensor(gated[:, tt, :], bank[:, tt, 0:D], gate_bc[:, D:2 * D], ALU.mult).then_inc(S["gated2"], 1)
                for tt in range(NT):
                    dve.wait_ge(S["gated2"], n * NT + tt + 1)
                    dve.tensor_tensor(x3[:, tt, :], xt(n, tt), gated[:, tt, :], ALU.add).then_inc(S["x3_out"], 1)

            def x3_turned(n):
                dve.wait_ge(S["t3_pe"], n + 1)
                dve.tensor_copy(x3T[:, 0:2, :].rearrange("p a n -> p (a n)"), bank[0:KP, 0, :])
                dve.tensor_copy(x3T[:, 2, :], bank[0:KP, 1, 0:N]).then_inc(S["x3t_out"], 1)

            def z_copy(n):
                dve.wait_ge(S["z_pe"], n + 1)
                dve.tensor_copy(z_sb, bank[0:R, 0, 0:N]).then_inc(S["z_out"], 1)

            def y_sum(n):
                for tt in range(NT):
                    dve.wait_ge(S["rot_pe"], n * NT + tt + 1)
                    dve.tensor_tensor(xt(n, tt), x3[:, tt, :], bank[:, tt, 0:D], ALU.add).then_inc(S["y_out"], 1)

            def attention(n, previous, following):
                if following is not None:
                    norm_stats(following, 0, S["stat1"], S["mv1"])
                    norm_apply(following, 0, S["rstd1"], S["xn1"])
                if previous is not None:
                    x3_turned(previous)
                    z_copy(previous)
                    y_sum(previous)
                normalize(n, 0)
                if following is not None:
                    h1(following)
                for g in range(1, HG):
                    normalize(n, g)

            def step(i, last_attention):
                x2(i)
                norm_stats(i, 1, S["stat2"], S["mv2"])
                qk_low(i + 1, 0)
                qk_low(i + 1, 1)
                norm_apply(i, 1, S["rstd2"], S["xn2"])
                for k in range(2, 6):
                    qk_low(i + 1, k)
                h2(i)
                v_out(i + 1)
                for h in range(H):
                    row_max(i + 1, h)
                neg_max(i + 1)
                x3_out(i)
                attention(i + 1, i, None if last_attention else i + 2)

            dve.wait_ge(S["x_first"], 16)
            norm_stats(0, 0, S["stat1"], S["mv1"])
            norm_apply(0, 0, S["rstd1"], S["xn1"])
            h1(0)
            for k in range(6):
                qk_low(0, k)
            v_out(0)
            for h in range(H):
                row_max(0, h)
            neg_max(0)
            dve.wait_ge(S["x_rest"], 16 * (B - 1))
            attention(0, None, 1)
            with dve.Fori(0, B - 2) as i:
                step(i, False)
            step(B - 2, True)
            x2(B - 1)
            norm_stats(B - 1, 1, S["stat2"], S["mv2"])
            norm_apply(B - 1, 1, S["rstd2"], S["xn2"])
            h2(B - 1)
            x3_out(B - 1)
            x3_turned(B - 1)
            z_copy(B - 1)
            y_sum(B - 1)


def layouts(a):
    def blocks(w, p=KP):
        w = np.asarray(w)
        return np.ascontiguousarray(w.reshape(-1, p, w.shape[-1]).transpose(1, 0, 2))

    f = np.float32
    o = {}
    o["x"] = np.ascontiguousarray(np.asarray(a["x"]).reshape(B, NT, P128, D).transpose(0, 2, 1, 3))
    o["condT"] = blocks(np.asarray(a["cond_1152"]).T)
    o["w_ada"] = blocks(a["L0_cond_w_ada"])
    b_ada = np.asarray(a["L0_cond_b_ada"]).reshape(6, KB, KP)
    o["b_ada"] = np.ascontiguousarray(b_ada[[KIND[m] for m in MOD]].reshape(-1, KP).T)
    gate = np.concatenate([b_ada[KIND["gate_a"]].reshape(-1), b_ada[KIND["gate_f"]].reshape(-1)])
    o["b_gate"] = np.ascontiguousarray(np.stack([gate] * B))
    order = []
    for qk in range(2):
        for i, nh in enumerate(HEADS):
            h0 = sum(HEADS[:i])
            order += [qk * D + (h0 + h) * HD + d for d in range(HD) for h in range(nh)]
    w_qkv = np.asarray(a["L0_cond_w_qkv"])
    o["w_qkv"] = blocks(np.concatenate([w_qkv[:, order], w_qkv[:, 2 * D:]], axis=1))
    b_qkv = np.asarray(a["L0_cond_b_qkv"])
    b_qk = np.zeros((P128, 6), f)
    for i in range(6):
        h0, nh = sum(HEADS[:i // 2]), HEADS[i // 2]
        c = i % 2 * D + h0 * HD
        b_qk[:nh * HD, i] = b_qkv[order[c:c + nh * HD]]
    o["b_qk"] = b_qk
    o["b_v"] = np.ascontiguousarray(b_qkv[2 * D:])
    w_proj = np.zeros((HG, GH, 32, D), f)
    w_proj[:, :, :HD] = np.asarray(a["L0_cond_w_proj"]).reshape(HG, GH, HD, D)
    w_proj[0, 0, HD] = np.asarray(a["L0_cond_b_proj"])
    o["w_proj"] = blocks(w_proj.reshape(HG * P128, D), P128)
    o["w_fc1"] = blocks(a["L0_cond_w_fc1"])
    o["b_fc1"] = np.ascontiguousarray(np.asarray(a["L0_cond_b_fc1"]).reshape(FT, P128).T)
    o["w_fc2"] = blocks(a["L0_cond_w_fc2"], P128)
    o["b_fc2"] = np.ascontiguousarray(np.asarray(a["L0_cond_b_fc2"]))
    o["P"] = blocks(a["L1_cond_P"])
    iu, ju = np.triu_indices(R, k=1)
    w = np.zeros((D, R, R), f)
    w[:, ju, iu] = np.asarray(a["L1_cond_W"]).T
    o["w_skew"] = np.ascontiguousarray(w.reshape(KB, KP, R, R).transpose(1, 0, 2, 3))
    b = np.zeros((R, R), f)
    b[iu, ju] = np.asarray(a["L1_cond_b"])
    o["b_skew"] = b
    o["ident"] = np.eye(P128, dtype=f)
    sel = np.zeros((P128, P128), f)
    for m in range(P128):
        sel[m // 32 * 32 + HD, m] = 1
    o["sel"] = sel
    o["striu"] = np.triu(np.ones((R, R), f), 1)
    o["rowmask"] = blocks(np.tril(np.ones((D, R), f)))
    o["thr"] = np.tile((2.0 ** np.arange(SQUARINGS)).astype(f), (R, 1))
    return o


def kernel(**inputs):
    import concourse.bacc as bacc
    from concourse.bass_utils import run_bass_kernel_spmd

    arrays = layouts(inputs)
    nc = bacc.Bacc("TRN2", target_bir_lowering=False, num_devices=1)
    t = {n: nc.dram_tensor("in_" + n, a.shape, mybir.dt.from_np(a.dtype), kind="ExternalInput").ap() for n, a in arrays.items()}
    t["y"] = nc.dram_tensor("y", (B, P128, NT, D), mybir.dt.float32, kind="ExternalOutput").ap()
    build(nc, t)
    r = run_bass_kernel_spmd(nc, [{"in_" + n: a for n, a in arrays.items()}], core_ids=[0])
    y = r.results[0]["y"]
    return np.ascontiguousarray(y.transpose(0, 2, 1, 3)).reshape(B, N, D)
```

```python
from contextlib import ExitStack

import numpy as np

import concourse.bass as bass
from concourse import mybir

B, N, D = 8, 256, 288
H = 16
HD = D // H
HID = 4 * D
R = 64
P128 = 128
KB, KP = 3, 96
NT = N // P128
FT = HID // P128
HG, GH = 4, 4
HEADS = [6, 5, 5]
STACK = 4 * HD
TAYLOR = 10
PER_SAMPLE_SQ = 3
SQUARINGS = (B - 1) * PER_SAMPLE_SQ
QR_STEPS = R // B
LN_EPS = 1e-6
KIND = {"shift_a": 0, "scale_a": 1, "gate_a": 2, "shift_f": 3, "scale_f": 4, "gate_f": 5}
MOD = ["shift_a", "scale_a", "shift_f", "scale_f"]
WCHUNK = 4
CHUNKS = R // WCHUNK
Q4 = B // 2


def at_least(engine, semaphore, value):
    if isinstance(value, int) and value <= 0:
        return
    engine.wait_ge(semaphore, value)


def by_register(engine, semaphore, value, passed):
    engine.wait_ge(semaphore, value)
    engine.sem_inc(passed, 1)


def build(nc, t):
    f32, f32r, i32 = mybir.dt.float32, mybir.dt.float32r, mybir.dt.int32
    ALU, ACT, AX = mybir.AluOpType, mybir.ActivationFunctionType, mybir.AxisListType
    ctx, setup_ctx = ExitStack(), ExitStack()
    with ctx:
        def sb(name, shape, dt=f32, where=ctx):
            return where.enter_context(nc.sbuf_tensor(name, shape, dt))

        def sem(name):
            return ctx.enter_context(nc.semaphore(name))

        ident = sb("ident", [P128, P128])
        sel = sb("sel", [P128, P128])
        wqkv_hi, wqkv_lo = sb("wqkv_hi", [KP, KB, 3 * D], f32r), sb("wqkv_lo", [KP, KB, 3 * D], f32r)
        wfc1_hi, wfc1_lo = sb("wfc1_hi", [KP, KB, HID], f32r), sb("wfc1_lo", [KP, KB, HID], f32r)
        wfc2_hi, wfc2_lo = sb("wfc2_hi", [P128, FT, D], f32r), sb("wfc2_lo", [P128, FT, D], f32r)
        wproj = sb("wproj", [P128, HG, D])
        bqk = sb("bqk", [P128, 6])
        bv = sb("bv", [P128, D])
        bfc1 = sb("bfc1", [P128, FT])
        bfc2 = sb("bfc2", [P128, D])
        mod = sb("mod", [KP, len(MOD) * KB, B])
        scond = sb("scond", [KP, KB, B])
        ones_r = sb("ones_r", [2, N], f32r)
        power = sb("power", [P128, 2])
        bskew = sb("bskew", [P128, R])
        thr = sb("thr", [P128, SQUARINGS])
        ones = sb("ones", [P128, R])
        eye2 = sb("eye2", [P128, R])
        striu = sb("striu", [R, R])
        bada = sb("bada", [KP, len(MOD) * KB])
        As, X, XT = (sb(n, [P128, Q4, R]) for n in ("As", "X", "XT"))
        keep = sb("keep", [P128, Q4, R], i32)
        norm1, scl = sb("norm1", [P128, Q4]), sb("scl", [P128, Q4])
        fi = sb("fi", [P128, SQUARINGS, Q4], i32)
        flags = keep[:].bitcast(f32).rearrange("p q r -> p (q r)")[:, 0:Q4 * SQUARINGS]\
            .rearrange("p (q k) -> p q k", q=Q4)
        rowmask = sb("rowmask", [KP, KB, R + 1])
        Pm = sb("Pm", [KP, KB, R + 1])
        Uh = sb("Uh", [KP, KB, R])
        pivot = sb("pivot", [KP, KB + 1])
        sr = sb("sr", [KP, 2 * R])
        small = sb("small", [KP, 12])
        wrow = sb("wrow", [KP, R])
        gates = sb("gates", [B, 2 * D])

        wada = sb("wada", [KP, KB, 6 * D], f32, setup_ctx)
        raw_qkv = sb("raw_qkv", [KP, KB, 3 * D], f32, setup_ctx)
        raw_fc1 = sb("raw_fc1", [KP, KB, HID], f32, setup_ctx)
        raw_fc2 = sb("raw_fc2", [P128, FT, D], f32, setup_ctx)
        setup_ctx.close()
        q_st = sb("q_st", [STACK + 2, H, N], f32r)
        k_st = sb("k_st", [STACK + 2, H, N], f32r)
        probs = sb("probs", [P128, 4, 2, NT, N])
        v_aug = sb("v_aug", [P128, NT, H, 32])
        o_nrm = sb("o_nrm", [P128, HG, N])

        skew_ctx = ExitStack()
        wskew = sb("wskew", [KP, 3, KB, WCHUNK, R], f32, skew_ctx)
        skew_ctx.close()
        NG = 3
        g32 = sb("g32", [P128, NG, N])
        g_hi, g_lo = sb("g_hi", [P128, NG, N], f32r), sb("g_lo", [P128, NG, N], f32r)

        xa = sb("xa", [P128, NT, D])
        xb = sb("xb", [P128, NT, D])
        xn = sb("xn", [P128, NT, D])
        stats = sb("stats", [P128, NT, 6])
        mv = sb("mv", [P128, 2, NT, 2])
        rstd = sb("rstd", [P128, 2, NT])
        h32 = sb("h32", [KP, KB, N])
        h1_hi, h1_lo = sb("h1_hi", [KP, KB, N], f32r), sb("h1_lo", [KP, KB, N], f32r)
        h2_hi, h2_lo = sb("h2_hi", [KP, KB, N], f32r), sb("h2_lo", [KP, KB, N], f32r)
        NS = 6
        qk_hi, qk_lo = sb("qk_hi", [6 * HD, NS, N], f32r), sb("qk_lo", [6 * HD, NS, N], f32r)
        o_raw = sb("o_raw", [P128, 2, N])
        o_inv = sb("o_inv", [P128, 2, N])
        rowmax = sb("rowmax", [P128, NT, H])
        nm_hi, nm_lo = sb("nm_hi", [H, N], f32r), sb("nm_lo", [H, N], f32r)
        gate_bc = sb("gate_bc", [P128, 2 * D])
        gb2 = sb("gb2", [P128, D])
        gated = sb("gated", [P128, 2, D])

        rot_out = probs[0:R, 0:3, :, :, :].rearrange("p a b c n -> p (a b c n)")[:, 0:B * D]\
            .rearrange("p (b d) -> p b d", b=B)
        late = probs[:, 3, :, :, :].rearrange("p b c n -> p (b c n)")
        U_q = late[0:KP, 0:KB * R].rearrange("p (a j) -> p a j", a=KB)
        QT = late[:, KB * R:KB * R + D]
        UhT = late[0:R, 512:512 + D]
        Gm, L, LT, ET, UT1, Xq = (o_nrm[0:R].rearrange("p g n -> p (g n)")[:, k * R:(k + 1) * R] for k in range(6))
        dcol = small[0:R, 10:12]
        x3T = (h32[:], g32[0:KP])
        z_sb = (gated[0:R, 0, 0:N], gated[0:R, 1, 0:N])
        x_fin = (xa, xb)

        bank = ctx.enter_context(nc.psum_tensor("bank", [P128, 8, 512], f32))

        gate_dram = nc.dram_tensor("gate_scratch", (B, 2 * D), f32).ap()
        x3_dram = nc.dram_tensor("x3_scratch", (B, P128, NT, D), f32).ap()

        names = """consts wada_in cond_in bias_in p_in qkv_in fc1_in fc2_in
        silu ada_pe gates_pe ada_out gates_out gates_stored hi_qkv hi_fc1 hi_fc2 lo_qkv split_out ones_set ones_in pool_set
        link setup_done skew_pe skew_out exp_pe exp_out exp_small keep_out passed passed_pe passed_pool
        pivot_out dots_pe sr_out root_out qr_link refl_out fac_pe fac_out
        xa_in xb_in x3_stored gate_in
        stat1 stat2 mv1 mv2 eps1 eps2 rstd1 rstd2 xn1 xn2 t1_pe t2_pe h32_1 h32_2 hhi1 hhi2 h1_out h2_out
        qk_pe qk_hi_out qk_lo_out v_pe v_out max_pe max_out maxt_pe nmhi_out nm_out nm_in
        st_pe prob_out pv_pe o_out bc_pe inv_out nrm_out proj_pe gated1 x2_out
        gb2_out x2b_out fc1_pe gelu_out ghi_out glo_out fc2k_pe gated2 x3_out
        fin_in0 fin_in1 t3_pe x3t_out x3t_rest z_pe z_out rot_pe y_out y_stored"""
        S = {n: sem(n) for n in names.split()}
        stack_in = [sem(f"stack_in{i}") for i in range(6)]
        wskew_in = [sem(f"wskew_in{i}") for i in range(3)]
        N_CONSTS = 8
        EXP_ROUNDS = TAYLOR + 2

        block = ctx.enter_context(nc.Block())

        @block.sync
        def _(sp):
            def load(dst, src, s):
                sp.dma_start(dst, src).then_inc(s, 16)
            load(scond[:], t["condT"], S["cond_in"])
            load(wada[:], t["w_ada"], S["wada_in"])
            load(bada[:], t["b_ada"], S["wada_in"])
            load(gates[:], t["b_gate"], S["wada_in"])
            load(xa[:], t["x"][0], S["xa_in"])
            load(ident[:], t["ident"], S["consts"])
            load(raw_qkv[:], t["w_qkv"], S["qkv_in"])
            load(sel[:], t["sel"], S["consts"])
            load(rowmask[:], t["rowmask"], S["consts"])
            load(thr[:], t["thr"], S["consts"])
            load(bskew[:], t["b_skew"], S["consts"])
            load(Pm[:], t["P"], S["consts"])
            load(eye2[:], t["eye2"], S["consts"])
            load(striu[:], t["striu"], S["consts"])
            load(bqk[:], t["b_qk"], S["bias_in"])
            load(bv[:], t["b_v"].partition_broadcast(P128), S["bias_in"])
            load(raw_fc1[:], t["w_fc1"], S["fc1_in"])
            load(raw_fc2[:], t["w_fc2"], S["fc2_in"])
            load(bfc1[:], t["b_fc1"], S["bias_in"])
            load(bfc2[:], t["b_fc2"].partition_broadcast(P128), S["bias_in"])
            load(wproj[:], t["w_proj"], S["bias_in"])
            load(xb[:], t["x"][0], S["xb_in"])

            def skew_load(c):
                if c >= 3:
                    sp.wait_ge(S["skew_pe"], c - 2)
                load(wskew[:, c % 3], t["w_skew"][:, :, c * WCHUNK:(c + 1) * WCHUNK, :], wskew_in[c % 3])

            for c in range(3):
                skew_load(c)
            sp.wait_ge(S["gates_out"], 1)
            load(gate_dram, gates[:], S["gates_stored"])
            sp.wait_ge(S["gates_stored"], 16)
            load(gate_bc[:], gate_dram[0, :].partition_broadcast(P128), S["gate_in"])
            sp.wait_ge(S["ones_set"], 1)
            sp.wait_ge(S["setup_done"], 1)
            load(k_st[STACK:STACK + 2, :, :].bitcast(f32), ones_r[:].bitcast(f32).unsqueeze(1).to_broadcast([2, H, N]),
                 S["ones_in"])

            def stack(n):
                at_least(sp, S["st_pe"], n * 8)
                for i in range(6):
                    h0, nh = sum(HEADS[:i // 2]), HEADS[i // 2]
                    dst = (q_st, k_st)[i % 2]
                    for low in range(2):
                        sp.wait_ge(S["qk_lo_out" if low else "qk_hi_out"], n * 6 + i + 1)
                        src = (qk_hi, qk_lo)[low]
                        for r in ((2 * low, 2 * low + 1) if i % 2 == 0 else (low, low + 2)):
                            sp.dma_start(dst[r * HD:(r + 1) * HD, h0:h0 + nh, :].bitcast(f32),
                                         src[0:nh * HD, i, :].bitcast(f32)).then_inc(stack_in[i], 16)

            def negmax(n):
                sp.wait_ge(S["nm_out"], n + 1)
                sp.dma_start(q_st[STACK:STACK + 1, :, :].bitcast(f32), nm_hi[:].bitcast(f32)).then_inc(S["nm_in"], 16)
                sp.dma_start(q_st[STACK + 1:STACK + 2, :, :].bitcast(f32), nm_lo[:].bitcast(f32)).then_inc(S["nm_in"], 16)

            def next_xa(n):
                sp.wait_ge(S["xn1"], n * NT)
                sp.dma_start(xa[:], t["x"][n]).then_inc(S["xa_in"], 16)

            def x3_to_scratch(n):
                sp.wait_ge(S["x3_out"], (n + 1) * NT)
                sp.dma_start(x3_dram[n], xb[:]).then_inc(S["x3_stored"], 16)

            def next_xb(n):
                sp.dma_start(gate_bc[:], gate_dram[bass.ds(n, 1), :].rearrange("o d -> (o d)")
                             .partition_broadcast(P128)).then_inc(S["gate_in"], 16)
                sp.wait_ge(S["x3_stored"], n * 16)
                sp.dma_start(xb[:], t["x"][n]).then_inc(S["xb_in"], 16)

            stack(0)
            next_xa(1)
            for c in range(3, CHUNKS):
                skew_load(c)
            negmax(0)

            def step(i, last_attention):
                stack(i + 1)
                if not last_attention:
                    next_xa(i + 2)
                negmax(i + 1)
                x3_to_scratch(i)
                next_xb(i + 1)

            with sp.Fori(0, B - 2) as i:
                step(i, False)
            step(B - 2, True)
            x3_to_scratch(B - 1)
            sp.wait_ge(S["x3_stored"], B * 16)

            def finish_load(n, u):
                at_least(sp, S["y_stored"], (n - 1) * 16)
                sp.dma_start(x_fin[u][:], x3_dram[n]).then_inc(S[f"fin_in{u}"], 16)

            def finish_store(n, u):
                sp.wait_ge(S["y_out"], (n + 1) * NT)
                sp.dma_start(t["y"][n], x_fin[u][:]).then_inc(S["y_stored"], 16)

            finish_load(0, 0)
            finish_load(1, 1)
            with sp.Fori(0, B // 2 - 1) as i:
                for u in range(2):
                    finish_store(2 * i + u, u)
                    sp.wait_ge(S["y_stored"], (2 * i + u + 1) * 16)
                    sp.dma_start(x_fin[u][:], x3_dram[2 * i + (u + 2)]).then_inc(S[f"fin_in{u}"], 16)
            finish_store(B - 2, 0)
            finish_store(B - 1, 1)
            sp.wait_ge(S["y_stored"], 16 * B)

        @block.tensor
        def _(pe):
            def mm(out, lhsT, rhs, start, stop):
                return pe.matmul(out, lhsT, rhs, start=start, stop=stop)

            def mm3(out, lhsT, rhs, start, stop):
                mm(out, lhsT[0], rhs[0], start, False)
                mm(out, lhsT[0], rhs[1], False, False)
                return mm(out, lhsT[1], rhs[0], False, stop)

            def ada():
                pe.wait_ge(S["silu"], 1)
                pe.wait_ge(S["wada_in"], 48)
                for m, name in enumerate(MOD):
                    for fb in range(KB):
                        c = KIND[name] * D + fb * KP
                        o = (m * KB + fb) * B
                        for kb in range(KB):
                            last = mm(bank[0:KP, 2, o:o + B], wada[:, kb, c:c + KP], scond[:, kb, :],
                                      kb == 0, kb == KB - 1)
                last.then_inc(S["ada_pe"], 1)
                for g, name in enumerate(("gate_a", "gate_f")):
                    for kb in range(KB):
                        last = mm(bank[0:B, 3 + g, 0:D], scond[:, kb, :],
                                  wada[:, kb, KIND[name] * D:(KIND[name] + 1) * D], kb == 0, kb == KB - 1)
                last.then_inc(S["gates_pe"], 1)

            def halves(out, lhsT, rhs):
                for f in range(2):
                    last = mm(out(slice(f * R, (f + 1) * R)), lhsT(slice(f * R, (f + 1) * R)),
                              rhs(slice(f * R, (f + 1) * R)), True, True)
                return last

            def skew(c):
                pe.wait_ge(wskew_in[c % 3], 16 * (c // 3 + 1))
                at_least(pe, S["skew_out"], c - 1)
                for jj in range(WCHUNK):
                    for kb in range(KB):
                        for f in range(2):
                            last = mm(bank[f * R:(f + 1) * R, 6 + c % 2, jj:Q4 * WCHUNK:WCHUNK],
                                      wskew[:, c % 3, kb, jj, :], scond[:, kb, f * Q4:(f + 1) * Q4],
                                      kb == 0, kb == KB - 1)
                last.then_inc(S["skew_pe"], 1)

            def per_sample(bk, o, lhsT, rhs):
                for q in range(Q4):
                    last = halves(lambda p: bank[p, bk, o + q * R:o + (q + 1) * R], lambda p: lhsT[p, q, :],
                                  lambda p: rhs[p, q, :])
                return last

            def turned(bk, src):
                for q in range(Q4):
                    last = halves(lambda p: bank[p, bk, q * R:(q + 1) * R], lambda p: src[p, q, :],
                                  lambda p: ident[p, p])
                return last

            def exp_round(k):
                if k == 0:
                    pe.wait_ge(S["skew_out"], CHUNKS)
                    last = turned(0, XT)
                else:
                    pe.wait_ge(S["exp_out"], k)
                    if k == 1:
                        last = halves(lambda p: bank[p, 0, 0:Q4 * R], lambda p: ones[p, :],
                                      lambda p: X[p].rearrange("p b j -> p (b j)"))
                    elif k < EXP_ROUNDS - 1:
                        last = per_sample(0, 0, As, X)
                    else:
                        last = turned(0, X)
                last.then_inc(S["exp_pe"], 1)

            def square(s):
                by_register(pe, S["exp_out"], s + EXP_ROUNDS, S["passed_pe"])
                per_sample(6, 0, XT, X)
                per_sample(6, Q4 * R, X, XT).then_inc(S["exp_pe"], 1)

            def qr(n, k, bk, o):
                pe.wait_ge(S["pivot_out"], n * QR_STEPS + (k + 1))
                for kb in range(KB):
                    mm(bank[0:KP, bk, o:o + R], pivot[:, kb:kb + 1].to_broadcast([KP, KP]), Pm[:, kb, 0:R],
                       kb == 0, kb == KB - 1)
                mm(bank[0:KP, bk, o + R:o + 2 * R], pivot[:, KB:KB + 1].to_broadcast([KP, KP]), Pm[:, 0, 0:R],
                   True, True).then_inc(S["dots_pe"], 1)

            def factor(k):
                pe.wait_ge(S["fac_out"], k + 1)
                if k == 0:
                    for kb in range(KB):
                        mm(bank[0:R, 6, 0:R], Uh[:, kb, :], Uh[:, kb, :], kb == 0, kb == KB - 1)
                    for kb in range(KB):
                        last = pe.transpose(bank[0:R, 7, kb * KP:(kb + 1) * KP], Uh[:, kb, :], ident[0:KP, 0:KP])
                elif k == 1:
                    last = pe.transpose(bank[0:R, 6, 0:R], L, ident[0:R, 0:R])
                elif k < 8:
                    if k < 7:
                        mm(bank[0:R, 6, 0:R], LT, L, True, True)
                        last = mm(bank[0:R, 6, R:2 * R], L, LT, True, True)
                    if k > 2:
                        last = mm(bank[0:R, 6, 2 * R:3 * R], L, ET, True, True)
                elif k == 8:
                    last = mm(bank[0:R, 6, 0:R], ET, UT1, True, True)
                elif k == 9:
                    for kb in range(KB):
                        mm(bank[0:KP, 6, kb * R:(kb + 1) * R], UhT[:, kb * KP:(kb + 1) * KP], Xq, True, True)
                    for f in range(2):
                        last = mm(bank[f * R:(f + 1) * R, 7, 0:D], Xq, UhT, True, True)
                else:
                    for q in range(Q4):
                        b = (k - 10) * Q4 + q
                        p = slice(b // Q4 * R, (b // Q4 + 1) * R)
                        last = mm(bank[0:R, 4 + q, 0:D], XT[p, q, :], QT[p, :], True, True)
                last.then_inc(S["fac_pe"], 1)

            def transpose_rows(bk, src, done):
                for kb in range(KB):
                    for tt in range(NT):
                        o = kb % 2 * N + tt * P128
                        last = pe.transpose(bank[0:KP, bk + kb // 2, o:o + P128], src[:, tt, kb * KP:(kb + 1) * KP],
                                            ident[:])
                last.then_inc(done, 1)

            def t1(n):
                pe.wait_ge(S["xn1"], (n + 1) * NT)
                transpose_rows(0, xn, S["t1_pe"])

            def qk(n, i):
                if i == 0:
                    pe.wait_ge(S["h1_out"], (n + 1) * KB)
                h0, nh = sum(HEADS[:i // 2]), HEADS[i // 2]
                c = i % 2 * D + h0 * HD
                if i >= 4:
                    pe.wait_ge(S["qk_lo_out"], n * 6 + i - 3)
                for kb in range(KB):
                    last = mm3(bank[0:nh * HD, 2 + i % 4, 0:N],
                               (wqkv_hi[:, kb, c:c + nh * HD], wqkv_lo[:, kb, c:c + nh * HD]),
                               (h1_hi[:, kb, :], h1_lo[:, kb, :]), kb == 0, kb == KB - 1)
                last.then_inc(S["qk_pe"], 1)

            def v(n):
                for tt in range(NT):
                    for kb in range(KB):
                        last = mm3(bank[:, tt, 0:D], (h1_hi[:, kb, tt * P128:(tt + 1) * P128],
                                                      h1_lo[:, kb, tt * P128:(tt + 1) * P128]),
                                   (wqkv_hi[:, kb, 2 * D:3 * D], wqkv_lo[:, kb, 2 * D:3 * D]), kb == 0, kb == KB - 1)
                    last.then_inc(S["v_pe"], 1)

            def max_scores(n, h):
                i = 0 if h < HEADS[0] else (1 if h < HEADS[0] + HEADS[1] else 2)
                if h in (0, HEADS[0], HEADS[0] + HEADS[1]):
                    pe.wait_ge(stack_in[2 * i], (n + 1) * 64)
                    pe.wait_ge(stack_in[2 * i + 1], (n + 1) * 64)
                if h >= 2:
                    pe.wait_ge(S["max_out"], n * H + h - 1)
                for tt in range(NT):
                    last = mm(bank[:, 4 + h % 2, tt * N:(tt + 1) * N], q_st[0:STACK, h, tt * P128:(tt + 1) * P128],
                              k_st[0:STACK, h, :], True, True)
                last.then_inc(S["max_pe"], 1)

            def max_transpose(n):
                pe.wait_ge(S["max_out"], (n + 1) * H)
                pe.wait_ge(S["sr_out"], n * QR_STEPS + 5)
                for tt in range(NT):
                    last = pe.transpose(bank[0:H, 7, tt * P128:(tt + 1) * P128], rowmax[:, tt, :], ident[:])
                last.then_inc(S["maxt_pe"], 1)

            def scores(n, i):
                if i == 0:
                    pe.wait_ge(S["nm_in"], (n + 1) * 32)
                    pe.wait_ge(S["ones_in"], 16)
                if i >= 2:
                    pe.wait_ge(S["prob_out"], n * 8 + i - 1)
                for hh in range(2):
                    for tt in range(NT):
                        last = mm(bank[:, 2 + i % 2 * 2 + hh, tt * N:(tt + 1) * N],
                                  k_st[:, 2 * i + hh, tt * P128:(tt + 1) * P128], q_st[:, 2 * i + hh, :], True, True)
                last.then_inc(S["st_pe"], 1)

            def pv(n, g):
                pe.wait_ge(S["prob_out"], n * 8 + 2 * g + 2)
                if g == 0:
                    pe.wait_ge(S["v_out"], (n + 1) * NT)
                    pe.wait_ge(S["nm_out"], n + 1)
                if g >= 2:
                    pe.wait_ge(S["inv_out"], n * HG + g - 1)
                for tt in range(NT):
                    for j in range(GH):
                        h = GH * g + j
                        last = mm(bank[32 * j:32 * j + 32, 6 + g % 2, 0:N], v_aug[:, tt, h, :],
                                  probs[:, h // 2 % 4, h % 2, tt, :], tt == 0, tt == NT - 1)
                last.then_inc(S["pv_pe"], 1)

            def sums(n, g):
                pe.wait_ge(S["o_out"], n * HG + g + 1)
                mm(bank[:, 6 + g % 2, N:2 * N], sel[:], o_raw[:, g % 2, :], True, True).then_inc(S["bc_pe"], 1)

            def proj(n):
                pe.wait_ge(S["nrm_out"], (n + 1) * HG)
                for tt in range(NT):
                    for g in range(HG):
                        last = mm(bank[:, tt, 0:D], o_nrm[:, g, tt * P128:(tt + 1) * P128], wproj[:, g, :],
                                  g == 0, g == HG - 1)
                    last.then_inc(S["proj_pe"], 1)

            def t2(n):
                pe.wait_ge(S["xn2"], (n + 1) * NT)
                transpose_rows(4, xn, S["t2_pe"])

            def fc1(n, j):
                if j == 0:
                    pe.wait_ge(S["h2_out"], (n + 1) * KB)
                if j >= 2:
                    pe.wait_ge(S["gelu_out"], n * FT + j - 1)
                for kb in range(KB):
                    last = mm3(bank[:, 2 + j % 2, 0:N],
                               (wfc1_hi[:, kb, j * P128:(j + 1) * P128], wfc1_lo[:, kb, j * P128:(j + 1) * P128]),
                               (h2_hi[:, kb, :], h2_lo[:, kb, :]), kb == 0, kb == KB - 1)
                last.then_inc(S["fc1_pe"], 1)

            def fc2(n, k):
                pe.wait_ge(S["glo_out"], n * FT + k + 1)
                for tt in range(NT):
                    last = mm3(bank[:, tt, 0:D], (g_hi[:, k % NG, tt * P128:(tt + 1) * P128],
                                                  g_lo[:, k % NG, tt * P128:(tt + 1) * P128]),
                               (wfc2_hi[:, k, :], wfc2_lo[:, k, :]), k == 0, k == FT - 1)
                last.then_inc(S["fc2k_pe"], 1)

            def attention(n, first, last_attention):
                def exp_of_first(*rounds):
                    for k in rounds if first else ():
                        exp_round(k)
                scores(n, 0)
                scores(n, 1)
                exp_of_first(0)
                if not first:
                    pe.wait_ge(S["x3_out"], n * NT)
                qr(n, 5, 1, 384)
                scores(n, 2)
                exp_of_first(1)
                scores(n, 3)
                exp_of_first(2)
                pv(n, 0)
                exp_of_first(3)
                scores(n, 4)
                exp_of_first(4)
                scores(n, 5)
                exp_of_first(5)
                pv(n, 1)
                exp_of_first(6)
                sums(n, 0)
                qr(n, 6, 1, 384)
                exp_of_first(7)
                scores(n, 6)
                if not last_attention:
                    if first:
                        pe.wait_ge(S["exp_out"], 8)
                    pe.wait_ge(S["sr_out"], n * QR_STEPS + 7)
                    t1(n + 1)
                scores(n, 7)
                if first:
                    pe.wait_ge(S["h32_1"], 2 * KB)
                exp_of_first(8, 9)
                pv(n, 2)
                exp_of_first(10)
                sums(n, 1)
                if not last_attention:
                    pe.wait_ge(S["h32_1"], (n + 2) * KB)
                qr(n, 7, 1, 384)
                exp_of_first(11)
                pv(n, 3)
                sums(n, 2)
                sums(n, 3)

            def step(i, last_attention):
                n = i + 1
                pe.wait_ge(S["inv_out"], n * HG)
                proj(i)
                qr(n, 0, 7, 0)
                for k in range(3):
                    qk(n, k)
                qr(n, 1, 7, 0)
                for k in range(3, 6):
                    qk(n, k)
                pe.wait_ge(S["qk_lo_out"], n * 6 + 4)
                t2(i)
                pe.wait_ge(S["x2_out"], (i + 1) * NT)
                v(n)
                qr(n, 2, 7, 0)
                pe.wait_ge(S["qk_lo_out"], n * 6 + 6)
                fc1(i, 0)
                for j in range(1, FT):
                    fc1(i, j)
                    if j == 2:
                        pe.wait_ge(S["v_out"], (n + 1) * NT)
                    if j >= 2:
                        fc2(i, j - 2)
                    max_scores(n, 2 * j - 2)
                    max_scores(n, 2 * j - 1)
                    if j in (2, 4):
                        qr(n, 2 + j // 2, 7, 0)
                    if j in (1, 3, 5):
                        square(i * PER_SAMPLE_SQ + j // 2)
                max_transpose(n)
                fc2(i, FT - 2)
                fc2(i, FT - 1)
                attention(n, False, last_attention)

            ada()
            pe.wait_ge(S["consts"], 16 * N_CONSTS)
            t1(0)
            pe.wait_ge(S["lo_qkv"], 1)
            pe.wait_ge(S["gates_out"], 1)
            for k in range(6):
                qk(0, k)
            v(0)
            pe.wait_ge(S["pool_set"], 1)
            pe.wait_ge(S["v_out"], NT)
            for c in range(CHUNKS):
                skew(c)
                if c == 0:
                    pe.wait_ge(S["qk_lo_out"], 6)
                max_scores(0, c)
                if c % 3 == 2:
                    qr(0, c // 3, 1, 384)
            pe.wait_ge(S["skew_out"], CHUNKS)
            max_transpose(0)
            attention(0, True, False)
            with pe.Fori(0, B - 2) as i:
                step(i, False)
            def last_step():
                i, n = B - 2, B - 1
                step(i, True)
            last_step()
            n = B - 1
            proj(n)
            t2(n)
            fc1(n, 0)
            pe.wait_ge(S["x2_out"], (n + 1) * NT)
            for j in range(1, FT):
                fc1(n, j)
                factor(j - 1)
                if j >= 2:
                    fc2(n, j - 2)
            factor(FT - 1)
            fc2(n, FT - 2)
            factor(FT)
            fc2(n, FT - 1)
            factor(FT + 1)
            factor(FT + 2)
            pe.wait_ge(S["fac_out"], FT + 4)
            with pe.Fori(0, B // 2) as i:
                for u in range(2):
                    pe.wait_ge(S[f"fin_in{u}"], i * 16 + 16)
                    transpose_rows(2 * u, x_fin[u], S["t3_pe"])
                for u in range(2):
                    pe.wait_ge(S["x3t_out"], i * 2 + (u + 1))
                    pe.wait_ge(S["x3t_rest"], i * 2 + (u + 1))
                    for kb in range(KB):
                        last = mm(bank[0:R, 2 * u + 1, N:2 * N], U_q[:, kb, :], x3T[u][:, kb, :], kb == 0, kb == KB - 1)
                    last.then_inc(S["z_pe"], 1)
                for u in range(2):
                    pe.wait_ge(S["z_out"], i * 2 + (u + 1))
                    for tt in range(NT):
                        mm(bank[:, 4 + 2 * u + tt, 0:D], z_sb[u][:, tt * P128:(tt + 1) * P128],
                           rot_out[:, bass.ds(i * 2 + u, 1), :].rearrange("p o d -> p (o d)"), True, True)\
                            .then_inc(S["rot_pe"], 1)

        @block.scalar
        def _(act):
            def split(raw, hi, arrived, done):
                act.wait_ge(S[arrived], 16)
                act.activation(hi[:], raw[:], ACT.Copy).then_inc(S[done], 1)

            def h1(n):
                for kb in range(KB):
                    act.wait_ge(S["h32_1"], n * KB + (kb + 1))
                    act.activation(h1_hi[:, kb, :], h32[:, kb, :], ACT.Copy).then_inc(S["hhi1"], 1)

            def qk(n):
                for i in range(6):
                    nh = HEADS[i // 2]
                    act.wait_ge(S["qk_pe"], n * 6 + i + 1)
                    at_least(act, stack_in[i], n * 64)
                    act.activation(qk_hi[0:nh * HD, i, :], bank[0:nh * HD, 2 + i % 4, 0:N], ACT.Identity,
                                   bias=bqk[0:nh * HD, i:i + 1]).then_inc(S["qk_hi_out"], 1)

            def h2(n):
                for kb in range(KB):
                    act.wait_ge(S["h32_2"], n * KB + kb + 1)
                    act.activation(h2_hi[:, kb, :], h32[:, kb, :], ACT.Copy).then_inc(S["hhi2"], 1)

            def exp(n, i):
                act.wait_ge(S["st_pe"], n * 8 + i + 1)
                at_least(act, S["pv_pe"], n * HG + i // 2 - 1 if i >= 4 else n * HG)
                act.activation(probs[:, i % 4].rearrange("p h t n -> p (h t n)"),
                               bank[:, 2 + i % 2 * 2:4 + i % 2 * 2, :].rearrange("p h n -> p (h n)"),
                               ACT.Exp, scale=float(HD) ** -0.5).then_inc(S["prob_out"], 1)

            def o_copy(n, g):
                act.wait_ge(S["pv_pe"], n * HG + g + 1)
                at_least(act, S["nrm_out"], n * HG + g - 1 if g >= 1 else n * HG)
                act.activation(o_raw[:, g % 2, :], bank[:, 6 + g % 2, 0:N], ACT.Copy).then_inc(S["o_out"], 1)

            def attention(n, last_attention):
                for i in range(4):
                    exp(n, i)
                o_copy(n, 0)
                exp(n, 4)
                exp(n, 5)
                o_copy(n, 1)
                exp(n, 6)
                exp(n, 7)
                o_copy(n, 2)
                if not last_attention:
                    h1(n + 1)
                o_copy(n, 3)

            def gelu(n):
                for j in range(FT):
                    act.wait_ge(S["fc1_pe"], n * FT + j + 1)
                    if j >= NG:
                        act.wait_ge(S["fc2k_pe"], n * FT + j - 2)
                    act.activation(g32[:, j % NG, :], bank[:, 2 + j % 2, 0:N], ACT.Gelu_apprx_tanh,
                                   bias=bfc1[:, j:j + 1]).then_inc(S["gelu_out"], 1)
                    act.wait_ge(S["gelu_out"], n * FT + j + 1)
                    act.activation(g_hi[:, j % NG, :], g32[:, j % NG, :], ACT.Copy).then_inc(S["ghi_out"], 1)

            def step(i, last_attention):
                qk(i + 1)
                h2(i)
                gelu(i)
                attention(i + 1, last_attention)

            act.wait_ge(S["cond_in"], 16)
            act.activation(scond[:], scond[:], ACT.Silu).then_inc(S["silu"], 1)
            split(raw_qkv, wqkv_hi, "qkv_in", "hi_qkv")
            h1(0)
            act.wait_ge(S["bias_in"], 16 * 5)
            qk(0)
            split(raw_fc1, wfc1_hi, "fc1_in", "hi_fc1")
            split(raw_fc2, wfc2_hi, "fc2_in", "hi_fc2")
            attention(0, False)
            with act.Fori(0, B - 2) as i:
                step(i, False)
            step(B - 2, True)
            h2(B - 1)
            gelu(B - 1)
            with act.Fori(0, B // 2) as i:
                for u in range(2):
                    act.wait_ge(S["t3_pe"], i * 2 + (u + 1))
                    act.activation(x3T[u][:, 2, :], bank[0:KP, 2 * u + 1, 0:N], ACT.Copy).then_inc(S["x3t_rest"], 1)
                for u in range(2):
                    act.wait_ge(S["z_pe"], i * 2 + (u + 1))
                    act.activation(z_sb[u], bank[0:R, 2 * u + 1, N:2 * N], ACT.Copy).then_inc(S["z_out"], 1)

        @block.gpsimd
        def _(pool):
            def rstd_of(w, n, mv_sem, eps_sem, out_sem):
                by_register(pool, mv_sem, (n + 1) * NT, S["passed_pool"])
                pool.tensor_scalar(rstd[:, w, :], mv[:, w, :, 1], LN_EPS, None, ALU.add).then_inc(eps_sem, 1)
                pool.wait_ge(eps_sem, n + 1)
                pool.tensor_tensor(rstd[:, w, :], rstd[:, w, :], power[:, 0:1].to_broadcast([P128, NT]),
                                   ALU.pow).then_inc(out_sem, 1)

            def root(n, k):
                pool.wait_ge(S["sr_out"], n * QR_STEPS + (k + 1))
                pool.tensor_tensor(small[:, 0:1], sr[:, bass.ds(n * QR_STEPS + k, 1)], power[0:KP, 1:2],
                                   ALU.pow).then_inc(S["root_out"], 1)

            def x2_bias(n):
                pool.wait_ge(S["gate_in"], (n + 1) * 16)
                pool.tensor_tensor(gb2[:], gate_bc[:, D:2 * D], bfc2[:], ALU.mult).then_inc(S["gb2_out"], 1)
                pool.wait_ge(S["gb2_out"], n + 1)
                pool.wait_ge(S["xn2"], (n + 1) * NT)
                pool.tensor_tensor(xb[:], xb[:], gb2[:].unsqueeze(1).to_broadcast([P128, NT, D]),
                                   ALU.add).then_inc(S["x2b_out"], 1)

            def g_low(n, j):
                pool.wait_ge(S["ghi_out"], n * FT + j + 1)
                pool.tensor_tensor(g_lo[:, j % NG, :], g32[:, j % NG, :], g_hi[:, j % NG, :].bitcast(f32),
                                   ALU.subtract).then_inc(S["glo_out"], 1)

            def normalize(n, g):
                pool.wait_ge(S["inv_out"], n * HG + (g + 1))
                pool.tensor_tensor(o_nrm[:, g, :], o_raw[:, g % 2, :], o_inv[:, g % 2, :],
                                   ALU.mult).then_inc(S["nrm_out"], 1)

            def attention(n, last_attention):
                if not last_attention:
                    rstd_of(0, n + 1, S["mv1"], S["eps1"], S["rstd1"])
                root(n, 5)
                normalize(n, 0)
                root(n, 6)
                normalize(n, 1)
                root(n, 7)
                normalize(n, 2)
                normalize(n, 3)

            def step(i, last_attention):
                n = i + 1
                root(n, 0)
                rstd_of(1, i, S["mv2"], S["eps2"], S["rstd2"])
                root(n, 1)
                x2_bias(i)
                root(n, 2)
                for j in range(FT):
                    g_low(i, j)
                    if j in (2, 4):
                        root(n, 2 + j // 2)
                attention(n, last_attention)

            pool.memset(ones[:], 1.0)
            pool.memset(power[:, 0:1], -0.5)
            pool.memset(power[:, 1:2], 0.5).then_inc(S["pool_set"], 1)
            pool.wait_ge(S["pool_set"], 1)
            rstd_of(0, 0, S["mv1"], S["eps1"], S["rstd1"])
            for k in range(5):
                root(0, k)
            attention(0, False)
            with pool.Fori(0, B - 2) as i:
                step(i, False)
            step(B - 2, True)
            rstd_of(1, B - 1, S["mv2"], S["eps2"], S["rstd2"])
            x2_bias(B - 1)
            for j in range(FT):
                g_low(B - 1, j)

        @block.vector
        def _(dve):
            links = [0]

            def link(ins):
                links[0] += 1
                ins.then_inc(S["link"], 1)
                dve.wait_ge(S["link"], links[0])

            def split_low(raw, hi, lo, done, out):
                dve.wait_ge(S[done], 1)
                dve.tensor_tensor(lo[:], raw[:], hi[:].bitcast(f32), ALU.subtract).then_inc(S[out], 1)

            eye_q = eye2[:].unsqueeze(1).to_broadcast([P128, Q4, R])

            def matrices(bk, o=0):
                return bank[:, bk, o:o + Q4 * R].rearrange("p (q j) -> p q j", j=R)

            def skew(c):
                cols = slice(c * WCHUNK, (c + 1) * WCHUNK)
                dve.wait_ge(S["skew_pe"], c + 1)
                dve.tensor_tensor(XT[:, :, cols], bank[:, 6 + c % 2, 0:Q4 * WCHUNK].rearrange("p (q j) -> p q j", q=Q4),
                                  bskew[:, cols].unsqueeze(1).to_broadcast([P128, Q4, WCHUNK]),
                                  ALU.add).then_inc(S["skew_out"], 1)

            def exp_round(k):
                dve.wait_ge(S["exp_pe"], k + 1)
                if k == 0:
                    link(dve.tensor_tensor(As[:], XT[:], matrices(0), ALU.subtract))
                    last = dve.scalar_tensor_tensor(X[:], As[:], -1.0, As[:], ALU.mult, ALU.max)
                elif k == 1:
                    thr_q = thr[:].unsqueeze(1).to_broadcast([P128, Q4, SQUARINGS])
                    link(dve.tensor_reduce(norm1[:], matrices(0), AX.X, ALU.max))
                    link(dve.tensor_tensor(flags, norm1[:].unsqueeze(2).to_broadcast([P128, Q4, SQUARINGS]), thr_q,
                                           ALU.is_gt))
                    link(dve.tensor_copy(fi[:], flags.rearrange("p q k -> p k q")))
                    link(dve.tensor_tensor(flags, flags, thr_q, ALU.mult))
                    link(dve.tensor_reduce(scl[:], flags, AX.X, ALU.add))
                    link(dve.tensor_scalar(scl[:], scl[:], 1.0, None, ALU.add))
                    link(dve.reciprocal(scl[:], scl[:]))
                    link(dve.tensor_tensor(As[:], As[:], scl[:].unsqueeze(2).to_broadcast([P128, Q4, R]), ALU.mult))
                    last = dve.scalar_tensor_tensor(X[:], As[:], 1.0 / TAYLOR, eye_q, ALU.mult, ALU.add)
                elif k < EXP_ROUNDS - 1:
                    last = dve.scalar_tensor_tensor(X[:], matrices(0), -1.0 / (TAYLOR + 1 - k), eye_q, ALU.mult, ALU.add)
                else:
                    last = dve.tensor_copy(XT[:], matrices(0))
                last.then_inc(S["exp_out"], 1)

            def square(s):
                dve.wait_ge(S["exp_out"], s + EXP_ROUNDS)
                dve.tensor_copy(keep[:], fi[:, bass.ds(s, 1), :].rearrange("p o q -> p (o q)").unsqueeze(2)
                                .to_broadcast([P128, Q4, R])).then_inc(S["keep_out"], 1)
                dve.wait_ge(S["keep_out"], s + 1)
                by_register(dve, S["exp_pe"], s + (EXP_ROUNDS + 1), S["passed"])
                dve.copy_predicated(X[:], keep[:], matrices(6))
                dve.copy_predicated(XT[:], keep[:], matrices(6, Q4 * R)).then_inc(S["exp_out"], 1)

            LINKS = 6
            gb, den, inv, hs = (small[:, c:c + 1] for c in (2, 3, 4, 5))

            def pivot_of(column):
                dve.tensor_tensor(pivot[:, 0:KB], Pm[:, :, column].rearrange("p a o -> p (a o)"),
                                  rowmask[:, :, column].rearrange("p a o -> p (a o)"), ALU.mult)
                dve.tensor_copy(pivot[:, KB:KB + 1], ident[0:KP, column]).then_inc(S["pivot_out"], 1)

            def qlink(n, k, at, ins):
                ins.then_inc(S["qr_link"], 1)
                dve.wait_ge(S["qr_link"], n * (QR_STEPS * LINKS) + (k * LINKS + at))

            QR_1, QR_7 = bank[0:KP, 1, 384:384 + 2 * R], bank[0:KP, 7, 0:2 * R]

            def qr_first(n, k, where):
                dve.wait_ge(S["dots_pe"], n * QR_STEPS + (k + 1))
                dve.tensor_copy(sr[:], where).then_inc(S["sr_out"], 1)
                dve.wait_ge(S["sr_out"], n * QR_STEPS + (k + 1))
                qlink(n, k, 1, dve.tensor_scalar(hs, sr[:, bass.ds(n * QR_STEPS + (k + R), 1)], 0.0, 0.5, ALU.is_ge,
                                                 ALU.subtract))

            def qr_second(n, k):
                j = n * QR_STEPS + k
                alpha, dot = sr[:, bass.ds(n * QR_STEPS + (k + R), 1)], sr[:, bass.ds(j, 1)]
                dve.wait_ge(S["root_out"], n * QR_STEPS + (k + 1))
                qlink(n, k, 2, dve.scalar_tensor_tensor(gb, hs, 2.0, small[:, 0:1], ALU.mult, ALU.mult))
                dve.scalar_tensor_tensor(wrow[:], sr[:, R:2 * R], gb, sr[:, 0:R], ALU.mult, ALU.add)
                dve.scalar_tensor_tensor(pivot[:, 0:1], pivot[:, KB:KB + 1], gb, pivot[:, 0:1], ALU.mult, ALU.add)
                qlink(n, k, 3, dve.scalar_tensor_tensor(den, alpha, gb, dot, ALU.mult, ALU.add))
                qlink(n, k, 4, dve.reciprocal(inv, den))
                qlink(n, k, 5, dve.tensor_scalar(small[:, 8:8 + KB], pivot[:, 0:KB], inv, -1.0, ALU.mult, ALU.mult))
                dve.tensor_copy(Uh[:, :, bass.ds(j, 1)].rearrange("p a o -> p (a o)"), pivot[:, 0:KB])
                for kb in range(KB):
                    last = dve.scalar_tensor_tensor(Pm[:, kb, 0:R], wrow[:], small[:, 8 + kb:9 + kb], Pm[:, kb, 0:R],
                                                    ALU.mult, ALU.add)
                qlink(n, k, 6, last)
                pivot_of(bass.ds(n * QR_STEPS + (k + 1), 1))

            eye1 = ident[0:R, 0:R]

            def factor(k):
                dve.wait_ge(S["fac_pe"], k + 1)
                if k == 0:
                    dve.tensor_copy(Gm, bank[0:R, 6, 0:R])
                    link(dve.tensor_copy(UhT, bank[0:R, 7, 0:D]))
                    link(dve.tensor_tensor(Xq, Gm, eye1, ALU.mult))
                    link(dve.tensor_reduce(dcol[:, 0:1], Xq, AX.X, ALU.add))
                    link(dve.tensor_scalar(dcol[:, 0:1], dcol[:, 0:1], 0.5, None, ALU.mult))
                    link(dve.reciprocal(dcol[:, 1:2], dcol[:, 0:1]))
                    link(dve.tensor_tensor(Gm, Gm, striu[:], ALU.mult))
                    dve.tensor_scalar(UT1, UhT[:, 0:R], dcol[:, 1:2], None, ALU.mult)
                    last = dve.tensor_scalar(L, Gm, dcol[:, 1:2], -1.0, ALU.mult, ALU.mult)
                elif k == 1:
                    link(dve.tensor_copy(LT, bank[0:R, 6, 0:R]))
                    last = dve.tensor_tensor(ET, LT, eye1, ALU.add)
                elif k < 8:
                    if k < 7:
                        dve.tensor_copy(L, bank[0:R, 6, 0:R])
                        last = dve.tensor_copy(LT, bank[0:R, 6, R:2 * R])
                    if k > 2:
                        last = dve.tensor_tensor(ET, ET, bank[0:R, 6, 2 * R:3 * R], ALU.add)
                elif k == 8:
                    last = dve.tensor_scalar(Xq, bank[0:R, 6, 0:R], -1.0, None, ALU.mult)
                elif k == 9:
                    dve.tensor_copy(U_q, bank[0:KP, 6, 0:KB * R].rearrange("p (a j) -> p a j", a=KB))
                    dve.tensor_tensor(XT[:], XT[:], eye_q, ALU.subtract)
                    link(dve.tensor_copy(QT, bank[:, 7, 0:D]))
                    dve.tensor_tensor(U_q[:, 0, :], U_q[:, 0, :], ident[0:KP, 0:R], ALU.add)
                    last = dve.tensor_tensor(QT[:, 0:R], QT[:, 0:R], eye2[:], ALU.add)
                else:
                    b = (k - 10) * Q4
                    last = dve.tensor_copy(rot_out[:, b:b + Q4, :], bank[0:R, 4:4 + Q4, 0:D])
                last.then_inc(S["fac_out"], 1)

            def norm_stats(n, w, x, stat_sem, mv_sem):
                for tt in range(NT):
                    if w == 0:
                        by_register(dve, S["xa_in"], (n + 1) * 16, S["passed"])
                    else:
                        by_register(dve, S["x2_out"], n * NT + tt + 1, S["passed"])
                    dve.bn_stats(stats[:, tt, :], x[:, tt, :]).then_inc(stat_sem, 1)
                for tt in range(NT):
                    by_register(dve, stat_sem, n * NT + tt + 1, S["passed"])
                    dve.bn_aggr(mv[:, w, tt, :], stats[:, tt, :]).then_inc(mv_sem, 1)

            def norm_apply(n, w, x, rstd_sem, out_sem):
                dve.wait_ge(rstd_sem, n + 1)
                for tt in range(NT):
                    dve.tensor_scalar(xn[:, tt, :], x[:, tt, :], mv[:, w, tt, 0:1], rstd[:, w, tt:tt + 1],
                                      ALU.subtract, ALU.mult).then_inc(out_sem, 1)

            def h32_of(n, kb, bk, m, out_sem):
                col = bass.ds(n, 1)
                dve.tensor_scalar(h32[:, kb, :], bank[0:KP, bk + kb // 2, kb % 2 * N:kb % 2 * N + N],
                                  mod[:, (m + 1) * KB + kb, col], mod[:, m * KB + kb, col],
                                  ALU.mult, ALU.add).then_inc(out_sem, 1)

            def h1(n):
                dve.wait_ge(S["t1_pe"], n + 1)
                for kb in range(KB):
                    h32_of(n, kb, 0, 0, S["h32_1"])

            def h1_low(n):
                for kb in range(KB):
                    dve.wait_ge(S["hhi1"], n * KB + kb + 1)
                    dve.tensor_tensor(h1_lo[:, kb, :], h32[:, kb, :], h1_hi[:, kb, :].bitcast(f32),
                                      ALU.subtract).then_inc(S["h1_out"], 1)

            def h2(n):
                dve.wait_ge(S["t2_pe"], n + 1)
                for kb in range(KB):
                    h32_of(n, kb, 4, 2, S["h32_2"])
                for kb in range(KB):
                    dve.wait_ge(S["hhi2"], n * KB + kb + 1)
                    dve.tensor_tensor(h2_lo[:, kb, :], h32[:, kb, :], h2_hi[:, kb, :].bitcast(f32),
                                      ALU.subtract).then_inc(S["h2_out"], 1)

            def qk_low(n, i):
                nh = HEADS[i // 2]
                dve.wait_ge(S["qk_hi_out"], n * 6 + i + 1)
                dve.scalar_tensor_tensor(qk_lo[0:nh * HD, i, :], bank[0:nh * HD, 2 + i % 4, 0:N],
                                         bqk[0:nh * HD, i:i + 1], qk_hi[0:nh * HD, i, :].bitcast(f32),
                                         ALU.add, ALU.subtract).then_inc(S["qk_lo_out"], 1)

            def v_out(n):
                for tt in range(NT):
                    dve.wait_ge(S["v_pe"], n * NT + tt + 1)
                    dve.tensor_tensor(v_aug[:, tt, :, 0:HD], bank[:, tt, 0:D].rearrange("p (h d) -> p h d", d=HD),
                                      bv[:].rearrange("p (h d) -> p h d", d=HD), ALU.add).then_inc(S["v_out"], 1)

            def row_max(n, h):
                dve.wait_ge(S["max_pe"], n * H + h + 1)
                dve.tensor_reduce(rowmax[:, :, h], bank[:, 4 + h % 2, :].rearrange("p (t m) -> p t m", t=NT),
                                  AX.X, ALU.max).then_inc(S["max_out"], 1)

            def neg_max(n):
                dve.wait_ge(S["maxt_pe"], n + 1)
                at_least(dve, S["nm_in"], n * 32)
                dve.tensor_scalar(nm_hi[:], bank[0:H, 7, 0:N], -1.0, None, ALU.mult).then_inc(S["nmhi_out"], 1)
                dve.wait_ge(S["nmhi_out"], n + 1)
                dve.scalar_tensor_tensor(nm_lo[:], bank[0:H, 7, 0:N], -1.0, nm_hi[:].bitcast(f32), ALU.mult,
                                         ALU.subtract).then_inc(S["nm_out"], 1)

            def inverse(n, g):
                dve.wait_ge(S["bc_pe"], n * HG + (g + 1))
                dve.reciprocal(o_inv[:, g % 2, :], bank[:, 6 + g % 2, N:2 * N]).then_inc(S["inv_out"], 1)

            def x2(n):
                dve.wait_ge(S["gate_in"], (n + 1) * 16)
                dve.wait_ge(S["xb_in"], (n + 1) * 16)
                for tt in range(NT):
                    dve.wait_ge(S["proj_pe"], n * NT + tt + 1)
                    dve.tensor_tensor(gated[:, tt, :], bank[:, tt, 0:D], gate_bc[:, 0:D], ALU.mult).then_inc(S["gated1"], 1)
                for tt in range(NT):
                    dve.wait_ge(S["gated1"], n * NT + tt + 1)
                    dve.tensor_tensor(xb[:, tt, :], xb[:, tt, :], gated[:, tt, :], ALU.add).then_inc(S["x2_out"], 1)

            def x3(n):
                dve.wait_ge(S["fc2k_pe"], (n + 1) * FT)
                dve.wait_ge(S["x2b_out"], n + 1)
                for tt in range(NT):
                    dve.tensor_tensor(gated[:, tt, :], bank[:, tt, 0:D], gate_bc[:, D:2 * D], ALU.mult).then_inc(S["gated2"], 1)
                for tt in range(NT):
                    dve.wait_ge(S["gated2"], n * NT + tt + 1)
                    dve.tensor_tensor(xb[:, tt, :], xb[:, tt, :], gated[:, tt, :], ALU.add).then_inc(S["x3_out"], 1)

            def attention(n, first, last_attention):
                def exp_of_first(*rounds):
                    for k in rounds if first else ():
                        exp_round(k)
                if not last_attention:
                    norm_stats(n + 1, 0, xa, S["stat1"], S["mv1"])
                    norm_apply(n + 1, 0, xa, S["rstd1"], S["xn1"])
                exp_of_first(0)
                qr_first(n, 5, QR_1)
                qr_second(n, 5)
                exp_of_first(1, 2, 3, 4, 5, 6)
                inverse(n, 0)
                qr_first(n, 6, QR_1)
                qr_second(n, 6)
                exp_of_first(7)
                if not last_attention:
                    h1(n + 1)
                exp_of_first(8, 9, 10)
                inverse(n, 1)
                qr_first(n, 7, QR_1)
                exp_of_first(11)
                if not last_attention:
                    h1_low(n + 1)
                inverse(n, 2)
                qr_second(n, 7)
                inverse(n, 3)

            def step(i, last_attention):
                n = i + 1
                x2(i)
                qr_first(n, 0, QR_7)
                norm_stats(i, 1, xb, S["stat2"], S["mv2"])
                qk_low(n, 0)
                qr_second(n, 0)
                qk_low(n, 1)
                norm_apply(i, 1, xb, S["rstd2"], S["xn2"])
                qk_low(n, 2)
                qr_first(n, 1, QR_7)
                qk_low(n, 3)
                qr_second(n, 1)
                qk_low(n, 4)
                qk_low(n, 5)
                h2(i)
                v_out(n)
                qr_first(n, 2, QR_7)
                for h in range(H):
                    row_max(n, h)
                    if h in (0, 4, 8):
                        qr_second(n, 2 + h // 4)
                    if h in (3, 7):
                        qr_first(n, 3 + h // 4, QR_7)
                    if h in (1, 5, 9):
                        square(i * PER_SAMPLE_SQ + h // 4)
                neg_max(n)
                x3(i)
                attention(n, False, last_attention)

            dve.memset(ones_r[:].bitcast(f32), 1.0).then_inc(S["ones_set"], 1)
            norm_stats(0, 0, xa, S["stat1"], S["mv1"])
            dve.wait_ge(S["wada_in"], 48)
            dve.wait_ge(S["ada_pe"], 1)
            link(dve.tensor_tensor(mod[:], bank[0:KP, 2, 0:len(MOD) * KB * B].rearrange("p (m b) -> p m b", b=B),
                                   bada[:].unsqueeze(2).to_broadcast([KP, len(MOD) * KB, B]), ALU.add))
            for m in (1, 3):
                link(dve.tensor_scalar(mod[:, m * KB:(m + 1) * KB, :], mod[:, m * KB:(m + 1) * KB, :], 1.0, None, ALU.add))
            dve.wait_ge(S["gates_pe"], 1)
            dve.tensor_tensor(gates[:].rearrange("p (g d) -> p g d", g=2), bank[0:B, 3:5, 0:D],
                              gates[:].rearrange("p (g d) -> p g d", g=2), ALU.add).then_inc(S["gates_out"], 1)
            norm_apply(0, 0, xa, S["rstd1"], S["xn1"])
            split_low(raw_qkv, wqkv_hi, wqkv_lo, "hi_qkv", "lo_qkv")
            h1(0)
            h1_low(0)
            dve.wait_ge(S["consts"], 16 * N_CONSTS)
            pivot_of(slice(0, 1))
            dve.wait_ge(S["bias_in"], 16 * 5)
            for k in range(6):
                qk_low(0, k)
            split_low(raw_fc1, wfc1_hi, wfc1_lo, "hi_fc1", "split_out")
            split_low(raw_fc2, wfc2_hi, wfc2_lo, "hi_fc2", "split_out")
            dve.wait_ge(S["split_out"], 2)
            dve.memset(v_aug[:], 1.0).then_inc(S["setup_done"], 1)
            dve.wait_ge(S["setup_done"], 1)
            v_out(0)
            for c in range(CHUNKS):
                skew(c)
                row_max(0, c)
                if c % 3 == 2:
                    qr_first(0, c // 3, QR_1)
                    qr_second(0, c // 3)
            neg_max(0)
            attention(0, True, False)
            with dve.Fori(0, B - 2) as i:
                step(i, False)
            step(B - 2, True)
            n = B - 1
            x2(n)
            norm_stats(n, 1, xb, S["stat2"], S["mv2"])
            norm_apply(n, 1, xb, S["rstd2"], S["xn2"])
            h2(n)
            dve.tensor_copy(small[0:1, 11:12], small[0:1, 0:1]).then_inc(S["fac_out"], 1)
            for k in range(FT + 3):
                factor(k)
                if k == FT:
                    x3_at = k
            x3(n)
            with dve.Fori(0, B // 2) as i:
                for u in range(2):
                    dve.wait_ge(S["t3_pe"], i * 2 + (u + 1))
                    dve.tensor_copy(x3T[u][:, 0:2, :].rearrange("p a n -> p (a n)"),
                                    bank[0:KP, 2 * u, :]).then_inc(S["x3t_out"], 1)
                for u in range(2):
                    for tt in range(NT):
                        dve.wait_ge(S["rot_pe"], i * 4 + (2 * u + tt + 1))
                        dve.tensor_tensor(x_fin[u][:, tt, :], x_fin[u][:, tt, :], bank[:, 4 + 2 * u + tt, 0:D],
                                          ALU.add).then_inc(S["y_out"], 1)


def layouts(a):
    def blocks(w, p=KP):
        w = np.asarray(w)
        return np.ascontiguousarray(w.reshape(-1, p, w.shape[-1]).transpose(1, 0, 2))

    f = np.float32
    o = {}
    o["x"] = np.ascontiguousarray(np.asarray(a["x"]).reshape(B, NT, P128, D).transpose(0, 2, 1, 3))
    o["condT"] = blocks(np.asarray(a["cond_1152"]).T)
    o["w_ada"] = blocks(a["L0_cond_w_ada"])
    b_ada = np.asarray(a["L0_cond_b_ada"]).reshape(6, KB, KP)
    o["b_ada"] = np.ascontiguousarray(b_ada[[KIND[m] for m in MOD]].reshape(-1, KP).T)
    gate = np.concatenate([b_ada[KIND["gate_a"]].reshape(-1), b_ada[KIND["gate_f"]].reshape(-1)])
    o["b_gate"] = np.ascontiguousarray(np.stack([gate] * B))
    order = []
    for qk in range(2):
        for i, nh in enumerate(HEADS):
            h0 = sum(HEADS[:i])
            order += [qk * D + (h0 + h) * HD + d for d in range(HD) for h in range(nh)]
    w_qkv = np.asarray(a["L0_cond_w_qkv"])
    o["w_qkv"] = blocks(np.concatenate([w_qkv[:, order], w_qkv[:, 2 * D:]], axis=1))
    b_qkv = np.asarray(a["L0_cond_b_qkv"])
    b_qk = np.zeros((P128, 6), f)
    for i in range(6):
        h0, nh = sum(HEADS[:i // 2]), HEADS[i // 2]
        c = i % 2 * D + h0 * HD
        b_qk[:nh * HD, i] = b_qkv[order[c:c + nh * HD]]
    o["b_qk"] = b_qk
    o["b_v"] = np.ascontiguousarray(b_qkv[2 * D:])
    w_proj = np.zeros((HG, GH, 32, D), f)
    w_proj[:, :, :HD] = np.asarray(a["L0_cond_w_proj"]).reshape(HG, GH, HD, D)
    w_proj[0, 0, HD] = np.asarray(a["L0_cond_b_proj"])
    o["w_proj"] = blocks(w_proj.reshape(HG * P128, D), P128)
    o["w_fc1"] = blocks(a["L0_cond_w_fc1"])
    o["b_fc1"] = np.ascontiguousarray(np.asarray(a["L0_cond_b_fc1"]).reshape(FT, P128).T)
    o["w_fc2"] = blocks(a["L0_cond_w_fc2"], P128)
    o["b_fc2"] = np.ascontiguousarray(np.asarray(a["L0_cond_b_fc2"]))
    o["P"] = blocks(np.concatenate([np.asarray(a["L1_cond_P"]), np.zeros((D, 1), f)], axis=1))
    iu, ju = np.triu_indices(R, k=1)
    w = np.zeros((D, R, R), f)
    w[:, ju, iu] = np.asarray(a["L1_cond_W"]).T
    o["w_skew"] = np.ascontiguousarray(w.reshape(KB, KP, R, R).transpose(1, 0, 2, 3))
    b = np.zeros((R, R), f)
    b[iu, ju] = np.asarray(a["L1_cond_b"])
    o["b_skew"] = np.concatenate([b, b])
    o["ident"] = np.eye(P128, dtype=f)
    sel = np.zeros((P128, P128), f)
    for m in range(P128):
        sel[m // 32 * 32 + HD, m] = 1
    o["sel"] = sel
    o["striu"] = np.triu(np.ones((R, R), f), 1)
    o["eye2"] = np.concatenate([np.eye(R, dtype=f), np.eye(R, dtype=f)])
    o["rowmask"] = blocks(np.tril(np.ones((D, R + 1), f)))
    o["thr"] = np.tile((2.0 ** np.arange(SQUARINGS)).astype(f), (P128, 1))
    return o


def kernel(**inputs):
    import concourse.bacc as bacc
    from concourse.bass_utils import run_bass_kernel_spmd

    arrays = layouts(inputs)
    nc = bacc.Bacc("TRN2", target_bir_lowering=False, num_devices=1)
    t = {n: nc.dram_tensor("in_" + n, a.shape, mybir.dt.from_np(a.dtype), kind="ExternalInput").ap() for n, a in arrays.items()}
    t["y"] = nc.dram_tensor("y", (B, P128, NT, D), mybir.dt.float32, kind="ExternalOutput").ap()
    build(nc, t)
    r = run_bass_kernel_spmd(nc, [{"in_" + n: a for n, a in arrays.items()}], core_ids=[0])
    y = r.results[0]["y"]
    return np.ascontiguousarray(y.transpose(0, 2, 1, 3)).reshape(B, N, D)
```

```python
from contextlib import ExitStack

import numpy as np

import concourse.bass as bass
from concourse import mybir

B, N, D = 8, 256, 288
H = 16
HD = D // H
HID = 4 * D
R = 64
P128 = 128
KB, KP = 3, 96
NT = N // P128
FT = HID // P128
HG, GH = 4, 4
HEADS = [6, 5, 5]
STACK = 4 * HD
TAYLOR = 10
PER_SAMPLE_SQ = 3
SQUARINGS = (B - 1) * PER_SAMPLE_SQ
QR_STEPS = R // B
LN_EPS = 1e-6
KIND = {"shift_a": 0, "scale_a": 1, "gate_a": 2, "shift_f": 3, "scale_f": 4, "gate_f": 5}
MOD = ["shift_a", "scale_a", "shift_f", "scale_f"]
FIRST_MAX_HEADS = [(), (0, 1), (2, 3), (4,), (5, 6), (7,), (8, 9), (10,), (11, 12), (13,), (14,), (15,)]
TRI = 16
TRI_AT = [sum(TRI * (R - TRI * m) for m in range(k)) for k in range(R // TRI + 1)]
WCHUNK = 256
CHUNKS = TRI_AT[-1] // WCHUNK
FACTOR_ROUNDS = 13
Q4 = B // 2


def at_least(engine, semaphore, value):
    if isinstance(value, int) and value <= 0:
        return
    engine.wait_ge(semaphore, value)


def by_register(engine, semaphore, value, passed):
    engine.wait_ge(semaphore, value)
    engine.sem_inc(passed, 1)


def build(nc, t):
    f32, f32r, i32 = mybir.dt.float32, mybir.dt.float32r, mybir.dt.int32
    ALU, ACT, AX = mybir.AluOpType, mybir.ActivationFunctionType, mybir.AxisListType
    ctx, setup_ctx = ExitStack(), ExitStack()
    with ctx:
        def sb(name, shape, dt=f32, where=ctx):
            return where.enter_context(nc.sbuf_tensor(name, shape, dt))

        def sem(name):
            return ctx.enter_context(nc.semaphore(name))

        ident = sb("ident", [P128, P128])
        sel = sb("sel", [P128, P128])
        wqkv_hi, wqkv_lo = sb("wqkv_hi", [KP, KB, 3 * D], f32r), sb("wqkv_lo", [KP, KB, 3 * D], f32r)
        wfc1_hi, wfc1_lo = sb("wfc1_hi", [KP, KB, HID], f32r), sb("wfc1_lo", [KP, KB, HID], f32r)
        wfc2_hi, wfc2_lo = sb("wfc2_hi", [P128, FT, D], f32r), sb("wfc2_lo", [P128, FT, D], f32r)
        wproj = sb("wproj", [P128, HG, D])
        bqk = sb("bqk", [P128, 6])
        bv = sb("bv", [P128, D])
        bfc1 = sb("bfc1", [P128, FT])
        bfc2 = sb("bfc2", [P128, D])
        mod = sb("mod", [KP, len(MOD) * KB, B])
        scond = sb("scond", [KP, KB, B])
        ones_r = sb("ones_r", [2, N], f32r)
        warm = sb("warm", [1, 1])
        power = sb("power", [P128, 2])
        bskew = sb("bskew", [P128, R])
        thr = sb("thr", [P128, SQUARINGS])
        ones = sb("ones", [P128, R])
        eye2 = sb("eye2", [P128, R])
        striu = sb("striu", [R, R])
        bada = sb("bada", [KP, len(MOD) * KB])
        As, X, XT = (sb(n, [P128, Q4, R]) for n in ("As", "X", "XT"))
        keep = sb("keep", [P128, Q4, R], i32)
        norm1, scl = sb("norm1", [P128, Q4]), sb("scl", [P128, Q4])
        fi = sb("fi", [P128, SQUARINGS, Q4], i32)
        flags = keep[:].bitcast(f32).rearrange("p q r -> p (q r)")[:, 0:Q4 * SQUARINGS]\
            .rearrange("p (q k) -> p q k", q=Q4)
        PT = sb("PT", [KP, D])
        upto = sb("upto", [R, R])
        below = sb("below", [R, R])
        e_j = sb("e_j", [KP, 1])
        u_j, products = sb("u_j", [R, D]), sb("products", [R, 2, D])
        G = sb("G", [R, R])
        small = sb("small", [R, 12])
        gates = sb("gates", [B, 2 * D])

        wada = sb("wada", [KP, KB, 6 * D], f32, setup_ctx)
        raw_qkv = sb("raw_qkv", [KP, KB, 3 * D], f32, setup_ctx)
        raw_fc1 = sb("raw_fc1", [KP, KB, HID], f32, setup_ctx)
        raw_fc2 = sb("raw_fc2", [P128, FT, D], f32, setup_ctx)
        setup_ctx.close()
        q_st = sb("q_st", [P128, H, N], f32r)
        k_st = sb("k_st", [STACK + 2, H, N], f32r)
        probs = sb("probs", [P128, 4, 2, NT, N])
        v_aug = sb("v_aug", [P128, NT, H, 32])
        o_nrm = sb("o_nrm", [P128, HG, N])

        skew_ctx = ExitStack()
        wskew = sb("wskew", [KP, 3, KB, WCHUNK], f32, skew_ctx)
        skew_ctx.close()
        NG = 3
        g32 = sb("g32", [P128, NG, N])
        g_hi, g_lo = sb("g_hi", [P128, NG, N], f32r), sb("g_lo", [P128, NG, N], f32r)

        xa = sb("xa", [P128, NT, D])
        xb = sb("xb", [P128, NT, D])
        xn = sb("xn", [P128, NT, D])
        stats = sb("stats", [P128, NT, 6])
        mv = sb("mv", [P128, 2, NT, 2])
        rstd = sb("rstd", [P128, 2, NT])
        h32 = sb("h32", [KP, KB, N])
        h1_hi, h1_lo = sb("h1_hi", [KP, KB, N], f32r), sb("h1_lo", [KP, KB, N], f32r)
        h2_hi, h2_lo = sb("h2_hi", [KP, KB, N], f32r), sb("h2_lo", [KP, KB, N], f32r)
        NS = 6
        qk_hi, qk_lo = sb("qk_hi", [6 * HD, NS, N], f32r), sb("qk_lo", [6 * HD, NS, N], f32r)
        o_raw = sb("o_raw", [P128, 2, N])
        o_inv = sb("o_inv", [P128, 2, NT, GH])
        rowmax = sb("rowmax", [P128, NT, H])
        nm_hi, nm_lo = sb("nm_hi", [H, N], f32r), sb("nm_lo", [H, N], f32r)
        gate_bc = sb("gate_bc", [P128, 2 * D])
        gb2 = sb("gb2", [P128, D])
        gated = sb("gated", [P128, 2, D])

        rot_out = probs[0:R, 0:3, :, :, :].rearrange("p a b c n -> p (a b c n)")[:, 0:B * D]\
            .rearrange("p (b d) -> p b d", b=B)
        late = probs[:, 3, :, :, :].rearrange("p b c n -> p (b c n)")
        U_q = late[0:KP, 0:KB * R].rearrange("p (a j) -> p a j", a=KB)
        QT = late[:, KB * R:KB * R + D]
        UhT = late[0:R, 512:512 + D]
        Uh = late[0:KP, 832:832 + KB * R].rearrange("p (a j) -> p a j", a=KB)
        Gm, L, LT, ET, UT1, Xq = (o_nrm[0:R].rearrange("p g n -> p (g n)")[:, k * R:(k + 1) * R] for k in range(6))
        dcol = small[0:R, 10:12]
        x3T = (h32[:], g32[0:KP])
        z_sb = (gated[0:R, 0, 0:N], gated[0:R, 1, 0:N])
        x_back = q_st[:].bitcast(f32).rearrange("p h n -> p (h n)")
        x_fin = [x_back[:, n * NT * D:(n + 1) * NT * D].rearrange("p (t d) -> p t d", t=NT) for n in range(B - 1)] + [xb]
        y_sb = (xa, xn)
        v_sb = (o_raw[0:B, 0, :], o_raw[0:B, 1, :], gated[0:B, 0, 0:N], gated[0:B, 1, 0:N])

        bank = ctx.enter_context(nc.psum_tensor("bank", [P128, 8, 512], f32))

        gate_dram = nc.dram_tensor("gate_scratch", (B, 2 * D), f32).ap()
        v_dram = nc.dram_tensor("v_scratch", (B, TRI_AT[-1]), f32).ap()
        x3_dram = nc.dram_tensor("x3_scratch", (B, P128, NT, D), f32).ap()

        names = """consts ident_in wada_in wada_rest cond_in bias_in qkv_in fc1_in fc2_in
        silu ada_pe gates_pe gates_out gates_stored hi_qkv hi_fc1 hi_fc2 lo_qkv split_out adab_pe ones_set ones_in pool_set
        link setup_done skew_pe v_copied xt_zero xt_in skew_out exp_pe exp_out keep_out passed passed_pe passed_pool
        pivot_out row_pe u_out norm_out root_out qr_link fac_pe fac_out
        xa_in xb_in x3_stored gate_in
        stat1 stat2 mv1 mv2 eps1 eps2 rstd1 rstd2 xn1 xn2 t1_pe t2_pe h32_1 h32_2 hhi1 hhi2 h1_out h2_out
        qk_pe qk_hi_out qk_lo_out v_pe v_out max_pe max_out maxt_pe nmhi_out nm_out nm_in
        st_pe prob_out pv_pe o_out sums_pe inv_out bc_pe nrm_out proj_pe gated1 x2_out
        gb2_out x2b_out fc1_pe gelu_out ghi_out glo_out fc2k_pe gated2 x3_out
        fin_in t3_pe x3t_out x3t_rest z_pe z_out rot_pe y_out"""
        S = {n: sem(n) for n in names.split()}
        y_stored = [sem(f"y_stored{i}") for i in range(2)]
        v_stored = [sem(f"v_stored{i}") for i in range(4)]
        stack_in = [sem(f"stack_in{i}") for i in range(6)]
        wskew_in = [sem(f"wskew_in{i}") for i in range(3)]
        N_CONSTS = 8
        EXP_ROUNDS = TAYLOR + 2

        block = ctx.enter_context(nc.Block())

        @block.sync
        def _(sp):
            def load(dst, src, s):
                sp.dma_start(dst, src).then_inc(s, 16)
            load(scond[:], t["condT"], S["cond_in"])
            load(wada[:, :, 0:2 * D], t["w_ada"][:, :, 0:2 * D], S["wada_in"])
            load(bada[:], t["b_ada"], S["wada_in"])
            load(xa[:], t["x"][0], S["xa_in"])
            load(ident[:], t["ident"], S["ident_in"])
            load(raw_qkv[:], t["w_qkv"], S["qkv_in"])
            load(wada[:, :, 2 * D:6 * D], t["w_ada"][:, :, 2 * D:6 * D], S["wada_rest"])
            load(gates[:], t["b_gate"], S["wada_rest"])
            load(raw_fc1[:], t["w_fc1"], S["fc1_in"])
            load(bqk[:], t["b_qk"], S["bias_in"])
            load(raw_fc2[:], t["w_fc2"], S["fc2_in"])
            load(PT[:], t["PT"], S["consts"])
            load(below[:], t["below"], S["consts"])
            load(upto[:], t["upto"], S["consts"])

            def skew_load(c):
                if c >= 3:
                    sp.wait_ge(S["skew_pe"], c - 2)
                load(wskew[:, c % 3], t["w_skew"][:, :, c * WCHUNK:(c + 1) * WCHUNK], wskew_in[c % 3])

            for c in range(3):
                skew_load(c)
            load(sel[:], t["sel"], S["consts"])
            load(thr[:], t["thr"], S["consts"])
            load(bskew[:], t["b_skew"], S["consts"])
            load(eye2[:], t["eye2"], S["consts"])
            load(striu[:], t["striu"], S["consts"])
            load(bv[:], t["b_v"].partition_broadcast(P128), S["bias_in"])
            load(bfc1[:], t["b_fc1"], S["bias_in"])
            load(bfc2[:], t["b_fc2"].partition_broadcast(P128), S["bias_in"])
            load(wproj[:], t["w_proj"], S["bias_in"])
            load(xb[:], t["x"][0], S["xb_in"])
            def triangle_load(m):
                for c in range(TRI_AT[m] // WCHUNK, TRI_AT[m + 1] // WCHUNK):
                    sp.wait_ge(v_stored[c % 4], (c // 4 + 1) * 16)
                for f in range(2):
                    load(XT[f * R + m * TRI:f * R + (m + 1) * TRI, :, m * TRI:R],
                         v_dram[f * Q4:(f + 1) * Q4, TRI_AT[m]:TRI_AT[m + 1]].rearrange("q (i j) -> i q j", i=TRI),
                         S["xt_in"])

            for c in range(3, CHUNKS):
                skew_load(c)
                if c == CHUNKS - 3:
                    sp.wait_ge(S["xt_zero"], 1)
                    triangle_load(0)
            for m in range(1, R // TRI):
                triangle_load(m)
            sp.wait_ge(S["gates_out"], 1)
            load(gate_dram, gates[:], S["gates_stored"])
            sp.wait_ge(S["gates_stored"], 16)
            load(gate_bc[:], gate_dram[0, :].partition_broadcast(P128), S["gate_in"])
            sp.wait_ge(S["ones_set"], 1)
            sp.wait_ge(S["setup_done"], 1)
            load(k_st[STACK:STACK + 2, :, :].bitcast(f32), ones_r[:].bitcast(f32).unsqueeze(1).to_broadcast([2, H, N]),
                 S["ones_in"])

            def stack(n):
                at_least(sp, S["st_pe"], n * 8)
                for i in range(6):
                    h0, nh = sum(HEADS[:i // 2]), HEADS[i // 2]
                    dst = (q_st, k_st)[i % 2]
                    for low in range(2):
                        sp.wait_ge(S["qk_lo_out" if low else "qk_hi_out"], n * 6 + i + 1)
                        src = (qk_hi, qk_lo)[low]
                        for r in ((2 * low, 2 * low + 1) if i % 2 == 0 else (low, low + 2)):
                            sp.dma_start(dst[r * HD:(r + 1) * HD, h0:h0 + nh, :].bitcast(f32),
                                         src[0:nh * HD, i, :].bitcast(f32)).then_inc(stack_in[i], 16)

            def negmax(n):
                sp.wait_ge(S["nmhi_out"], n + 1)
                sp.dma_start(q_st[STACK:STACK + 1, :, :].bitcast(f32), nm_hi[:].bitcast(f32)).then_inc(S["nm_in"], 16)
                sp.wait_ge(S["nm_out"], n + 1)
                sp.dma_start(q_st[STACK + 1:STACK + 2, :, :].bitcast(f32), nm_lo[:].bitcast(f32)).then_inc(S["nm_in"], 16)

            def next_xa(n):
                sp.wait_ge(S["xn1"], n * NT)
                sp.dma_start(xa[:], t["x"][n]).then_inc(S["xa_in"], 16)

            def x3_to_scratch(n):
                sp.wait_ge(S["x3_out"], (n + 1) * NT)
                sp.dma_start(x3_dram[n], xb[:]).then_inc(S["x3_stored"], 16)

            def next_xb(n):
                sp.dma_start(gate_bc[:], gate_dram[bass.ds(n, 1), :].rearrange("o d -> (o d)")
                             .partition_broadcast(P128)).then_inc(S["gate_in"], 16)
                sp.wait_ge(S["x3_stored"], n * 16)
                sp.dma_start(xb[:], t["x"][n]).then_inc(S["xb_in"], 16)

            stack(0)
            next_xa(1)
            negmax(0)

            def step(i, last_attention):
                stack(i + 1)
                if not last_attention:
                    next_xa(i + 2)
                negmax(i + 1)
                x3_to_scratch(i)
                next_xb(i + 1)

            with sp.Fori(0, B - 2) as i:
                step(i, False)
            step(B - 2, True)
            sp.wait_ge(S["st_pe"], B * 8)
            for n in range(B - 1):
                load(x_fin[n], x3_dram[n], S["fin_in"])
            for n in range(B):
                sp.wait_ge(S["y_out"], (n + 1) * NT)
                load(t["y"][n], y_sb[n % 2][:], y_stored[n % 2])
            for u in range(2):
                sp.wait_ge(y_stored[u], 16 * B // 2)

        @block.tensor
        def _(pe):
            def mm(out, lhsT, rhs, start, stop):
                return pe.matmul(out, lhsT, rhs, start=start, stop=stop)

            def mm3(out, lhsT, rhs, start, stop):
                mm(out, lhsT[0], rhs[0], start, False)
                mm(out, lhsT[0], rhs[1], False, False)
                return mm(out, lhsT[1], rhs[0], False, stop)

            def ada(m0, done):
                for m in range(m0, m0 + 2):
                    for fb in range(KB):
                        c = KIND[MOD[m]] * D + fb * KP
                        o = (m * KB + fb) * B
                        for kb in range(KB):
                            last = mm(bank[0:KP, 2 + m0 // 2, o:o + B], wada[:, kb, c:c + KP], scond[:, kb, :],
                                      kb == 0, kb == KB - 1)
                last.then_inc(S[done], 1)

            def gate_rows():
                for g, name in enumerate(("gate_a", "gate_f")):
                    for kb in range(KB):
                        last = mm(bank[0:B, 4 + g, 0:D], scond[:, kb, :],
                                  wada[:, kb, KIND[name] * D:(KIND[name] + 1) * D], kb == 0, kb == KB - 1)
                last.then_inc(S["gates_pe"], 1)

            def halves(out, lhsT, rhs):
                for f in range(2):
                    last = mm(out(slice(f * R, (f + 1) * R)), lhsT(slice(f * R, (f + 1) * R)),
                              rhs(slice(f * R, (f + 1) * R)), True, True)
                return last

            def skew(c):
                pe.wait_ge(wskew_in[c % 3], 16 * (c // 3 + 1))
                at_least(pe, S["v_copied"], c - 1)
                for kb in range(KB):
                    last = mm(bank[0:B, 6 + c % 2, 0:WCHUNK], scond[:, kb, :], wskew[:, c % 3, kb, :],
                              kb == 0, kb == KB - 1)
                last.then_inc(S["skew_pe"], 1)

            def per_sample(bk, o, lhsT, rhs):
                for q in range(Q4):
                    last = halves(lambda p: bank[p, bk, o + q * R:o + (q + 1) * R], lambda p: lhsT[p, q, :],
                                  lambda p: rhs[p, q, :])
                return last

            def turned(bk, src):
                for q in range(Q4):
                    last = halves(lambda p: bank[p, bk, q * R:(q + 1) * R], lambda p: src[p, q, :],
                                  lambda p: ident[p, p])
                return last

            def exp_round(k):
                if k == 0:
                    pe.wait_ge(S["skew_out"], 1)
                    last = turned(6, XT)
                else:
                    pe.wait_ge(S["exp_out"], k)
                    if k == 1:
                        last = halves(lambda p: bank[p, 6, 0:Q4 * R], lambda p: ones[p, :],
                                      lambda p: X[p].rearrange("p b j -> p (b j)"))
                    elif k < EXP_ROUNDS - 1:
                        last = per_sample(6, 0, As, X)
                    else:
                        last = turned(6, X)
                last.then_inc(S["exp_pe"], 1)

            def square(s):
                by_register(pe, S["exp_out"], s + EXP_ROUNDS, S["passed_pe"])
                per_sample(6, 0, XT, X)
                per_sample(6, Q4 * R, X, XT).then_inc(S["exp_pe"], 1)

            def qr(n, k, bk):
                pe.wait_ge(S["pivot_out"], n * QR_STEPS + (k + 1))
                mm(bank[0:R, bk, 0:D], e_j[:].to_broadcast([KP, R]), PT[:], True, True).then_inc(S["row_pe"], 1)

            def row_used(n, k):
                pe.wait_ge(S["u_out"], n * QR_STEPS + k)

            def factor(k):
                pe.wait_ge(S["fac_out"], k + 1)
                if k == 0:
                    for kb in range(KB):
                        last = pe.transpose(bank[0:KP, 6, kb * R:(kb + 1) * R], UhT[:, kb * KP:(kb + 1) * KP],
                                            ident[0:R, 0:R])
                elif k == 1:
                    for kb in range(KB):
                        last = mm(bank[0:R, 6, 0:R], Uh[:, kb, :], Uh[:, kb, :], kb == 0, kb == KB - 1)
                elif k == 2:
                    last = pe.transpose(bank[0:R, 6, 0:R], L, ident[0:R, 0:R])
                elif k < 9:
                    if k < 8:
                        mm(bank[0:R, 6, 0:R], LT, L, True, True)
                        last = mm(bank[0:R, 6, R:2 * R], L, LT, True, True)
                    if k > 3:
                        last = mm(bank[0:R, 6, 2 * R:3 * R], L, ET, True, True)
                elif k == 9:
                    last = mm(bank[0:R, 6, 0:R], ET, UT1, True, True)
                elif k == 10:
                    for kb in range(KB):
                        mm(bank[0:KP, 6, kb * R:(kb + 1) * R], UhT[:, kb * KP:(kb + 1) * KP], Xq, True, True)
                    for f in range(2):
                        last = mm(bank[f * R:(f + 1) * R, 7, 0:D], Xq, UhT, True, True)
                else:
                    for q in range(Q4):
                        b = (k - 11) * Q4 + q
                        p = slice(b // Q4 * R, (b // Q4 + 1) * R)
                        last = mm(bank[0:R, 4 + q, 0:D], XT[p, q, :], QT[p, :], True, True)
                last.then_inc(S["fac_pe"], 1)

            def transpose_rows(bk, src, done):
                for kb in range(KB):
                    for tt in range(NT):
                        o = kb % 2 * N + tt * P128
                        last = pe.transpose(bank[0:KP, bk + kb // 2, o:o + P128], src[:, tt, kb * KP:(kb + 1) * KP],
                                            ident[:])
                last.then_inc(done, 1)

            def t1(n):
                pe.wait_ge(S["xn1"], (n + 1) * NT)
                transpose_rows(0, xn, S["t1_pe"])

            def qk(n, i):
                if i == 0:
                    pe.wait_ge(S["h1_out"], (n + 1) * KB)
                h0, nh = sum(HEADS[:i // 2]), HEADS[i // 2]
                c = i % 2 * D + h0 * HD
                if i >= 4:
                    pe.wait_ge(S["qk_lo_out"], n * 6 + i - 3)
                for kb in range(KB):
                    last = mm3(bank[0:nh * HD, 2 + i % 4, 0:N],
                               (wqkv_hi[:, kb, c:c + nh * HD], wqkv_lo[:, kb, c:c + nh * HD]),
                               (h1_hi[:, kb, :], h1_lo[:, kb, :]), kb == 0, kb == KB - 1)
                last.then_inc(S["qk_pe"], 1)

            def v(n):
                for tt in range(NT):
                    for kb in range(KB):
                        last = mm3(bank[:, tt, 0:D], (h1_hi[:, kb, tt * P128:(tt + 1) * P128],
                                                      h1_lo[:, kb, tt * P128:(tt + 1) * P128]),
                                   (wqkv_hi[:, kb, 2 * D:3 * D], wqkv_lo[:, kb, 2 * D:3 * D]), kb == 0, kb == KB - 1)
                    last.then_inc(S["v_pe"], 1)

            def max_scores(n, h):
                i = 0 if h < HEADS[0] else (1 if h < HEADS[0] + HEADS[1] else 2)
                if h in (0, HEADS[0], HEADS[0] + HEADS[1]):
                    pe.wait_ge(stack_in[2 * i], (n + 1) * 64)
                    pe.wait_ge(stack_in[2 * i + 1], (n + 1) * 64)
                if h >= 2:
                    pe.wait_ge(S["max_out"], n * H + h - 1)
                for tt in range(NT):
                    last = mm(bank[:, 4 + h % 2, tt * N:(tt + 1) * N], q_st[0:STACK, h, tt * P128:(tt + 1) * P128],
                              k_st[0:STACK, h, :], True, True)
                last.then_inc(S["max_pe"], 1)

            def max_transpose(n):
                pe.wait_ge(S["max_out"], (n + 1) * H)
                row_used(n, 4)
                for tt in range(NT):
                    last = pe.transpose(bank[0:H, 7, tt * P128:(tt + 1) * P128], rowmax[:, tt, :], ident[:])
                last.then_inc(S["maxt_pe"], 1)

            def scores(n, i):
                if i == 0:
                    pe.wait_ge(S["nm_in"], (n + 1) * 32)
                    pe.wait_ge(S["ones_in"], 16)
                if i >= 2:
                    pe.wait_ge(S["prob_out"], n * 8 + i - 1)
                for hh in range(2):
                    for tt in range(NT):
                        last = mm(bank[:, 2 + i % 2 * 2 + hh, tt * N:(tt + 1) * N],
                                  k_st[:, 2 * i + hh, tt * P128:(tt + 1) * P128], q_st[0:STACK + 2, 2 * i + hh, :], True, True)
                last.then_inc(S["st_pe"], 1)

            def pv(n, g):
                pe.wait_ge(S["prob_out"], n * 8 + 2 * g + 2)
                if g == 0:
                    pe.wait_ge(S["v_out"], (n + 1) * NT)
                    pe.wait_ge(S["exp_out"], n * PER_SAMPLE_SQ + EXP_ROUNDS)
                    pe.wait_ge(S["nm_out"], n + 1)
                if g == 1:
                    row_used(n, 6)
                if g >= 2:
                    pe.wait_ge(S["nrm_out"], n * HG + g - 1)
                for tt in range(NT):
                    for j in range(GH):
                        h = GH * g + j
                        last = mm(bank[32 * j:32 * j + 32, 6 + g % 2, 0:N], v_aug[:, tt, h, :],
                                  probs[:, h // 2 % 4, h % 2, tt, :], tt == 0, tt == NT - 1)
                last.then_inc(S["pv_pe"], 1)

            def sums(n, g):
                pe.wait_ge(S["o_out"], n * HG + (g + 1))
                for tt in range(NT):
                    last = mm(bank[:, 6 + g % 2, N + tt * GH:N + (tt + 1) * GH],
                              o_raw[:, g % 2, tt * P128:(tt + 1) * P128], sel[:, 0:P128:32], True, True)
                last.then_inc(S["sums_pe"], 1)

            def spread(n, g):
                pe.wait_ge(S["inv_out"], n * HG + (g + 1))
                for tt in range(NT):
                    for j in range(GH):
                        last = mm(bank[32 * j:32 * j + 32, 6 + g % 2, N + tt * P128:N + (tt + 1) * P128],
                                  o_inv[:, g % 2, tt, j:j + 1].to_broadcast([P128, 32]), ident[:], True, True)
                last.then_inc(S["bc_pe"], 1)

            def proj(n):
                pe.wait_ge(S["nrm_out"], (n + 1) * HG)
                for tt in range(NT):
                    for g in range(HG):
                        last = mm(bank[:, tt, 0:D], o_nrm[:, g, tt * P128:(tt + 1) * P128], wproj[:, g, :],
                                  g == 0, g == HG - 1)
                    last.then_inc(S["proj_pe"], 1)

            def t2(n):
                pe.wait_ge(S["xn2"], (n + 1) * NT)
                transpose_rows(4, xn, S["t2_pe"])

            def fc1(n, j):
                if j == 0:
                    pe.wait_ge(S["h2_out"], (n + 1) * KB)
                if j >= 2:
                    pe.wait_ge(S["gelu_out"], n * FT + j - 1)
                for kb in range(KB):
                    last = mm3(bank[:, 2 + j % 2, 0:N],
                               (wfc1_hi[:, kb, j * P128:(j + 1) * P128], wfc1_lo[:, kb, j * P128:(j + 1) * P128]),
                               (h2_hi[:, kb, :], h2_lo[:, kb, :]), kb == 0, kb == KB - 1)
                last.then_inc(S["fc1_pe"], 1)

            def fc2(n, k):
                pe.wait_ge(S["glo_out"], n * FT + k + 1)
                for tt in range(NT):
                    last = mm3(bank[:, tt, 0:D], (g_hi[:, k % NG, tt * P128:(tt + 1) * P128],
                                                  g_lo[:, k % NG, tt * P128:(tt + 1) * P128]),
                               (wfc2_hi[:, k, :], wfc2_lo[:, k, :]), k == 0, k == FT - 1)
                last.then_inc(S["fc2k_pe"], 1)

            def attention(n, last_attention):
                pe.wait_ge(S["nm_out"], n + 1)
                qr(n, 4, 7)
                for i in range(4):
                    scores(n, i)
                pv(n, 0)
                scores(n, 4)
                if not last_attention:
                    t1(n + 1)
                qr(n, 5, 7)
                scores(n, 5)
                sums(n, 0)
                pv(n, 1)
                scores(n, 6)
                spread(n, 0)
                scores(n, 7)
                sums(n, 1)
                if last_attention:
                    pe.wait_ge(S["x3_out"], n * NT)
                else:
                    pe.wait_ge(S["h32_1"], (n + 2) * KB)
                qr(n, 6, 1)
                pv(n, 2)
                spread(n, 1)
                sums(n, 2)
                pv(n, 3)
                spread(n, 2)
                sums(n, 3)

            MAX_HEADS = [(), (0, 1), (2, 3, 4), (5, 6), (7, 8, 9), (10, 11), (12, 13), (14, 15), ()]

            def step(i, last_attention):
                n = i + 1
                qk(n, 0)
                spread(i, 3)
                qk(n, 1)
                pe.wait_ge(S["nrm_out"], n * HG)
                qr(i, 7, 7)
                row_used(i, 7)
                proj(i)
                qk(n, 2)
                qk(n, 3)
                qr(n, 0, 7)
                qk(n, 4)
                qk(n, 5)
                pe.wait_ge(S["qk_lo_out"], n * 6 + 4)
                t2(i)
                pe.wait_ge(S["x2_out"], (i + 1) * NT)
                v(n)
                pe.wait_ge(S["qk_lo_out"], n * 6 + 6)
                fc1(i, 0)
                for j in range(1, FT):
                    fc1(i, j)
                    if j == FT - 1:
                        max_transpose(n)
                    if j == 2:
                        pe.wait_ge(S["v_out"], (n + 1) * NT)
                    for h in MAX_HEADS[j][:1]:
                        max_scores(n, h)
                    if j >= 2:
                        fc2(i, j - 2)
                    for h in MAX_HEADS[j][1:2]:
                        max_scores(n, h)
                    if j in (1, 3, 5):
                        qr(n, 1 + j // 2, 7)
                    if j in (2, 4, 6):
                        square(i * PER_SAMPLE_SQ + (j // 2 - 1))
                    for h in MAX_HEADS[j][2:]:
                        max_scores(n, h)
                fc2(i, FT - 2)
                fc2(i, FT - 1)
                attention(n, last_attention)

            pe.wait_ge(S["silu"], 1)
            pe.wait_ge(S["wada_in"], 32)
            ada(0, "ada_pe")
            pe.wait_ge(S["ident_in"], 16)
            t1(0)
            pe.wait_ge(S["wada_rest"], 32)
            ada(2, "adab_pe")
            gate_rows()
            pe.wait_ge(S["lo_qkv"], 1)
            pe.wait_ge(S["gates_out"], 1)
            for c in range(CHUNKS):
                skew(c)
            pe.wait_ge(S["v_copied"], CHUNKS)
            qk(0, 0)
            qk(0, 1)
            qr(0, 0, 7)
            for k in range(2, 6):
                qk(0, k)
            pe.wait_ge(S["pool_set"], 1)
            exp_round(0)
            v(0)
            pe.wait_ge(S["qk_lo_out"], 6)
            pe.wait_ge(S["setup_done"], 1)
            for k in range(1, EXP_ROUNDS):
                exp_round(k)
                if k in (3, 5, 7):
                    qr(0, k // 2, 7)
                for h in FIRST_MAX_HEADS[k]:
                    max_scores(0, h)
            max_transpose(0)
            attention(0, False)
            with pe.Fori(0, B - 2) as i:
                step(i, False)
            step(B - 2, True)
            n = B - 1
            spread(n, 3)
            pe.wait_ge(S["nrm_out"], B * HG)
            qr(n, 7, 7)
            row_used(n, 7)
            proj(n)
            factor(0)
            t2(n)
            factor(1)
            fc1(n, 0)
            factor(2)
            pe.wait_ge(S["x2_out"], (n + 1) * NT)
            for j in range(1, FT):
                fc1(n, j)
                factor(j + 2)
                if j >= 2:
                    fc2(n, j - 2)
            fc2(n, FT - 2)
            factor(FT + 2)
            fc2(n, FT - 1)
            factor(FT + 3)
            def x3_turn(n):
                if n == 0:
                    pe.wait_ge(S["fin_in"], 16 * (B - 1))
                if n == B - 1:
                    pe.wait_ge(S["x3_out"], B * NT)
                transpose_rows(2 * (n % 2), x_fin[n], S["t3_pe"])

            def subspace(n):
                pe.wait_ge(S["x3t_out"], n + 1)
                pe.wait_ge(S["x3t_rest"], n + 1)
                for kb in range(KB):
                    last = mm(bank[0:R, 4 + n % 2, 0:N], U_q[:, kb, :], x3T[n % 2][:, kb, :], kb == 0, kb == KB - 1)
                last.then_inc(S["z_pe"], 1)

            def rotate(n):
                pe.wait_ge(S["z_out"], n + 1)
                at_least(pe, S["y_out"], n * NT)
                for tt in range(NT):
                    mm(bank[:, 6 + tt, 0:D], z_sb[n % 2][:, tt * P128:(tt + 1) * P128], rot_out[:, n, :],
                       True, True).then_inc(S["rot_pe"], 1)

            pe.wait_ge(S["x3_out"], B * NT)
            x3_turn(0)
            x3_turn(1)
            pe.wait_ge(S["fac_out"], FACTOR_ROUNDS + 1)
            for n in range(B):
                subspace(n)
                if n >= 1:
                    rotate(n - 1)
                if n + 2 < B:
                    x3_turn(n + 2)
            rotate(B - 1)

        @block.scalar
        def _(act):
            def split(raw, hi, arrived, done):
                act.wait_ge(S[arrived], 16)
                act.activation(hi[:], raw[:], ACT.Copy).then_inc(S[done], 1)

            def h1(n):
                for kb in range(KB):
                    act.wait_ge(S["h32_1"], n * KB + (kb + 1))
                    act.activation(h1_hi[:, kb, :], h32[:, kb, :], ACT.Copy).then_inc(S["hhi1"], 1)

            def qk(n, tiles=range(6)):
                for i in tiles:
                    nh = HEADS[i // 2]
                    act.wait_ge(S["qk_pe"], n * 6 + i + 1)
                    at_least(act, stack_in[i], n * 64)
                    act.activation(qk_hi[0:nh * HD, i, :], bank[0:nh * HD, 2 + i % 4, 0:N], ACT.Identity,
                                   bias=bqk[0:nh * HD, i:i + 1]).then_inc(S["qk_hi_out"], 1)

            def pivot_row(n, k, bk):
                act.wait_ge(S["row_pe"], n * QR_STEPS + (k + 1))
                act.activation(u_j[:], bank[0:R, bk, 0:D], ACT.Copy).then_inc(S["u_out"], 1)
                act.wait_ge(S["u_out"], n * QR_STEPS + (k + 1))
                act.activation(products[:, 0, :], u_j[:], ACT.Square,
                               accum_out=small[:, 1:2]).then_inc(S["norm_out"], 1)

            def h2(n):
                for kb in range(KB):
                    act.wait_ge(S["h32_2"], n * KB + kb + 1)
                    act.activation(h2_hi[:, kb, :], h32[:, kb, :], ACT.Copy).then_inc(S["hhi2"], 1)

            def exp(n, i):
                act.wait_ge(S["st_pe"], n * 8 + i + 1)
                at_least(act, S["pv_pe"], n * HG + i // 2 - 1 if i >= 4 else n * HG)
                act.activation(probs[:, i % 4].rearrange("p h t n -> p (h t n)"),
                               bank[:, 2 + i % 2 * 2:4 + i % 2 * 2, :].rearrange("p h n -> p (h n)"),
                               ACT.Exp, scale=float(HD) ** -0.5).then_inc(S["prob_out"], 1)

            def o_copy(n, g):
                act.wait_ge(S["pv_pe"], n * HG + g + 1)
                at_least(act, S["nrm_out"], n * HG + g - 1 if g >= 1 else n * HG)
                act.activation(o_raw[:, g % 2, :], bank[:, 6 + g % 2, 0:N], ACT.Copy).then_inc(S["o_out"], 1)

            def attention(n, last_attention):
                pivot_row(n, 4, 7)
                for i in range(4):
                    exp(n, i)
                o_copy(n, 0)
                exp(n, 4)
                pivot_row(n, 5, 7)
                exp(n, 5)
                if not last_attention:
                    h1(n + 1)
                o_copy(n, 1)
                exp(n, 6)
                exp(n, 7)
                pivot_row(n, 6, 1)
                o_copy(n, 2)
                o_copy(n, 3)

            def gelu(n, following):
                for j in range(FT):
                    act.wait_ge(S["fc1_pe"], n * FT + j + 1)
                    if j >= NG:
                        act.wait_ge(S["fc2k_pe"], n * FT + j - 2)
                    act.activation(g32[:, j % NG, :], bank[:, 2 + j % 2, 0:N], ACT.Gelu_apprx_tanh,
                                   bias=bfc1[:, j:j + 1]).then_inc(S["gelu_out"], 1)
                    act.wait_ge(S["gelu_out"], n * FT + j + 1)
                    act.activation(g_hi[:, j % NG, :], g32[:, j % NG, :], ACT.Copy).then_inc(S["ghi_out"], 1)
                    if following is not None and j in (1, 3, 5):
                        pivot_row(following, 1 + j // 2, 7)

            def step(i, last_attention):
                n = i + 1
                qk(n, range(2))
                pivot_row(i, 7, 7)
                qk(n, range(2, 4))
                pivot_row(n, 0, 7)
                qk(n, range(4, 6))
                h2(i)
                gelu(i, n)
                act.activation(warm[:], power[0:1, 0:1], ACT.Exp)
                attention(n, last_attention)

            act.wait_ge(S["cond_in"], 16)
            act.activation(scond[:], scond[:], ACT.Silu).then_inc(S["silu"], 1)
            split(raw_qkv, wqkv_hi, "qkv_in", "hi_qkv")
            h1(0)
            split(raw_fc1, wfc1_hi, "fc1_in", "hi_fc1")
            split(raw_fc2, wfc2_hi, "fc2_in", "hi_fc2")
            for c in range(CHUNKS):
                act.wait_ge(S["skew_pe"], c + 1)
                if c >= 4:
                    act.wait_ge(v_stored[c % 4], c // 4 * 16)
                act.activation(v_sb[c % 4], bank[0:B, 6 + c % 2, 0:WCHUNK], ACT.Copy).then_inc(S["v_copied"], 1)
                act.wait_ge(S["v_copied"], c + 1)
                act.dma_start(v_dram[:, c * WCHUNK:(c + 1) * WCHUNK], v_sb[c % 4]).then_inc(v_stored[c % 4], 16)
            act.wait_ge(S["bias_in"], 16 * 5)
            qk(0, range(2))
            pivot_row(0, 0, 7)
            qk(0, range(2, 6))
            for k in range(1, 4):
                pivot_row(0, k, 7)
            attention(0, False)
            with act.Fori(0, B - 2) as i:
                step(i, False)
            step(B - 2, True)
            pivot_row(B - 1, 7, 7)
            h2(B - 1)
            gelu(B - 1, None)
            def x3_turned(n):
                act.wait_ge(S["t3_pe"], n + 1)
                if n >= 2:
                    act.wait_ge(S["z_pe"], n - 1)
                act.activation(x3T[n % 2][:, 2, :], bank[0:KP, 2 * (n % 2) + 1, 0:N], ACT.Copy).then_inc(S["x3t_rest"], 1)

            x3_turned(0)
            x3_turned(1)
            for n in range(B):
                act.wait_ge(S["z_pe"], n + 1)
                if n >= 2:
                    act.wait_ge(S["rot_pe"], (n - 1) * NT)
                act.activation(z_sb[n % 2], bank[0:R, 4 + n % 2, 0:N], ACT.Copy).then_inc(S["z_out"], 1)
                if n + 2 < B:
                    x3_turned(n + 2)

        @block.gpsimd
        def _(pool):
            def rstd_of(w, n, mv_sem, eps_sem, out_sem):
                by_register(pool, mv_sem, (n + 1) * NT, S["passed_pool"])
                pool.tensor_scalar(rstd[:, w, :], mv[:, w, :, 1], LN_EPS, None, ALU.add).then_inc(eps_sem, 1)
                pool.wait_ge(eps_sem, n + 1)
                pool.tensor_tensor(rstd[:, w, :], rstd[:, w, :], power[:, 0:1].to_broadcast([P128, NT]),
                                   ALU.pow).then_inc(out_sem, 1)

            def root(n, k):
                pool.wait_ge(S["norm_out"], n * QR_STEPS + (k + 1))
                pool.tensor_tensor(small[:, 0:1], small[:, 1:2], power[0:R, 1:2],
                                   ALU.pow).then_inc(S["root_out"], 1)

            def x2_bias(n):
                pool.wait_ge(S["gate_in"], (n + 1) * 16)
                pool.tensor_tensor(gb2[:], gate_bc[:, D:2 * D], bfc2[:], ALU.mult).then_inc(S["gb2_out"], 1)
                pool.wait_ge(S["gb2_out"], n + 1)
                pool.wait_ge(S["xn2"], (n + 1) * NT)
                pool.tensor_tensor(xb[:], xb[:], gb2[:].unsqueeze(1).to_broadcast([P128, NT, D]),
                                   ALU.add).then_inc(S["x2b_out"], 1)

            def g_low(n, j):
                pool.wait_ge(S["ghi_out"], n * FT + j + 1)
                pool.tensor_tensor(g_lo[:, j % NG, :], g32[:, j % NG, :], g_hi[:, j % NG, :].bitcast(f32),
                                   ALU.subtract).then_inc(S["glo_out"], 1)

            def attention(n, last_attention):
                root(n, 4)
                if not last_attention:
                    rstd_of(0, n + 1, S["mv1"], S["eps1"], S["rstd1"])
                root(n, 5)
                root(n, 6)

            def step(i, last_attention):
                n = i + 1
                root(i, 7)
                rstd_of(1, i, S["mv2"], S["eps2"], S["rstd2"])
                root(n, 0)
                x2_bias(i)
                for j in range(FT):
                    g_low(i, j)
                    if j in (1, 3, 5):
                        root(n, 1 + j // 2)
                attention(n, last_attention)

            pool.memset(ones[:], 1.0)
            pool.memset(XT[:], 0.0).then_inc(S["xt_zero"], 1)
            pool.memset(power[:, 0:1], -0.5)
            pool.memset(power[:, 1:2], 0.5).then_inc(S["pool_set"], 1)
            pool.wait_ge(S["pool_set"], 1)
            rstd_of(0, 0, S["mv1"], S["eps1"], S["rstd1"])
            for k in range(4):
                root(0, k)
            attention(0, False)
            with pool.Fori(0, B - 2) as i:
                step(i, False)
            step(B - 2, True)
            root(B - 1, 7)
            rstd_of(1, B - 1, S["mv2"], S["eps2"], S["rstd2"])
            x2_bias(B - 1)
            for j in range(FT):
                g_low(B - 1, j)

        @block.vector
        def _(dve):
            links = [0]

            def link(ins):
                links[0] += 1
                ins.then_inc(S["link"], 1)
                dve.wait_ge(S["link"], links[0])

            def split_low(raw, hi, lo, done, out):
                dve.wait_ge(S[done], 1)
                dve.tensor_tensor(lo[:], raw[:], hi[:].bitcast(f32), ALU.subtract).then_inc(S[out], 1)

            eye_q = eye2[:].unsqueeze(1).to_broadcast([P128, Q4, R])

            def matrices(bk, o=0):
                return bank[:, bk, o:o + Q4 * R].rearrange("p (q j) -> p q j", j=R)

            def skew_bias():
                dve.wait_ge(S["xt_in"], R // TRI * 2 * 16)
                dve.tensor_tensor(XT[:], XT[:], bskew[:].unsqueeze(1).to_broadcast([P128, Q4, R]),
                                  ALU.add).then_inc(S["skew_out"], 1)
                dve.wait_ge(S["skew_out"], 1)

            def exp_round(k):
                dve.wait_ge(S["exp_pe"], k + 1)
                if k == 0:
                    link(dve.tensor_tensor(As[:], XT[:], matrices(6), ALU.subtract))
                    last = dve.scalar_tensor_tensor(X[:], As[:], -1.0, As[:], ALU.mult, ALU.max)
                elif k == 1:
                    thr_q = thr[:].unsqueeze(1).to_broadcast([P128, Q4, SQUARINGS])
                    link(dve.tensor_reduce(norm1[:], matrices(6), AX.X, ALU.max))
                    link(dve.tensor_tensor(flags, norm1[:].unsqueeze(2).to_broadcast([P128, Q4, SQUARINGS]), thr_q,
                                           ALU.is_gt))
                    link(dve.tensor_copy(fi[:], flags.rearrange("p q k -> p k q")))
                    link(dve.tensor_tensor(flags, flags, thr_q, ALU.mult))
                    link(dve.tensor_reduce(scl[:], flags, AX.X, ALU.add))
                    link(dve.tensor_scalar(scl[:], scl[:], 1.0, None, ALU.add))
                    link(dve.reciprocal(scl[:], scl[:]))
                    link(dve.tensor_tensor(As[:], As[:], scl[:].unsqueeze(2).to_broadcast([P128, Q4, R]), ALU.mult))
                    last = dve.scalar_tensor_tensor(X[:], As[:], 1.0 / TAYLOR, eye_q, ALU.mult, ALU.add)
                elif k < EXP_ROUNDS - 1:
                    last = dve.scalar_tensor_tensor(X[:], matrices(6), -1.0 / (TAYLOR + 1 - k), eye_q, ALU.mult, ALU.add)
                else:
                    last = dve.tensor_copy(XT[:], matrices(6))
                last.then_inc(S["exp_out"], 1)

            def square(s):
                dve.wait_ge(S["exp_out"], s + EXP_ROUNDS)
                dve.tensor_copy(keep[:], fi[:, bass.ds(s, 1), :].rearrange("p o q -> p (o q)").unsqueeze(2)
                                .to_broadcast([P128, Q4, R])).then_inc(S["keep_out"], 1)
                dve.wait_ge(S["keep_out"], s + 1)
                by_register(dve, S["exp_pe"], s + (EXP_ROUNDS + 1), S["passed"])
                dve.copy_predicated(X[:], keep[:], matrices(6))
                dve.copy_predicated(XT[:], keep[:], matrices(6, Q4 * R)).then_inc(S["exp_out"], 1)

            LINKS = 6
            norm2, s_j, hs, w_j, den, inv, c_j = (small[:, c:c + 1] for c in range(1, 8))

            def qlink(n, k, at, ins):
                ins.then_inc(S["qr_link"], 1)
                dve.wait_ge(S["qr_link"], n * (QR_STEPS * LINKS) + (k * LINKS + at))

            def qr_first(n, k):
                dve.wait_ge(S["u_out"], n * QR_STEPS + (k + 1))
                dve.scalar_tensor_tensor(products[:, 1, :], PT[0:R, :], 1.0, u_j[:], ALU.mult, ALU.mult, accum_out=s_j)
                qlink(n, k, 1, dve.tensor_scalar(hs, u_j[:, bass.ds(n * QR_STEPS + k, 1)], 0.0, 0.5, ALU.is_ge,
                                                 ALU.subtract))

            def qr_second(n, k):
                jcol = bass.ds(n * QR_STEPS + k, 1)
                gb = G[:, jcol]
                dve.wait_ge(S["root_out"], n * QR_STEPS + (k + 1))
                qlink(n, k, 2, dve.scalar_tensor_tensor(gb, hs, 2.0, small[:, 0:1], ALU.mult, ALU.mult))
                dve.scalar_tensor_tensor(den, u_j[:, jcol], gb, norm2, ALU.mult, ALU.add)
                qlink(n, k, 3, dve.scalar_tensor_tensor(w_j, PT[0:R, jcol], gb, s_j, ALU.mult, ALU.add))
                dve.tensor_tensor(u_j[:, jcol], u_j[:, jcol], gb, ALU.add)
                qlink(n, k, 4, dve.reciprocal(inv, den))
                qlink(n, k, 5, dve.scalar_tensor_tensor(c_j, w_j, inv, below[:, jcol], ALU.mult, ALU.mult))
                dve.tensor_copy(e_j[:], ident[0:KP, bass.ds(n * QR_STEPS + (k + 1), 1)])
                qlink(n, k, 6, dve.scalar_tensor_tensor(PT[0:R, :], u_j[:], c_j, PT[0:R, :], ALU.mult, ALU.add))
                dve.tensor_tensor(PT[0:R, jcol], PT[0:R, jcol], upto[:, jcol], ALU.mult).then_inc(S["pivot_out"], 1)

            eye1 = ident[0:R, 0:R]

            def reflectors():
                dve.wait_ge(S["pivot_out"], R + 1)
                link(dve.tensor_copy(UhT, PT[0:R, :]))
                link(dve.tensor_tensor(products[:, 0, 0:R], G[:], eye1, ALU.mult))
                dve.tensor_tensor(UhT[:, 0:R], UhT[:, 0:R], products[:, 0, 0:R], ALU.add).then_inc(S["fac_out"], 1)
                dve.wait_ge(S["fac_out"], 1)

            def factor(k):
                dve.wait_ge(S["fac_pe"], k + 1)
                if k == 0:
                    last = dve.tensor_copy(Uh.rearrange("p a j -> p (a j)"), bank[0:KP, 6, 0:KB * R])
                elif k == 1:
                    link(dve.tensor_copy(Gm, bank[0:R, 6, 0:R]))
                    link(dve.tensor_tensor(Xq, Gm, eye1, ALU.mult))
                    link(dve.tensor_reduce(dcol[:, 0:1], Xq, AX.X, ALU.add))
                    link(dve.tensor_scalar(dcol[:, 0:1], dcol[:, 0:1], 0.5, None, ALU.mult))
                    link(dve.reciprocal(dcol[:, 1:2], dcol[:, 0:1]))
                    link(dve.tensor_tensor(Gm, Gm, striu[:], ALU.mult))
                    dve.tensor_scalar(UT1, UhT[:, 0:R], dcol[:, 1:2], None, ALU.mult)
                    last = dve.tensor_scalar(L, Gm, dcol[:, 1:2], -1.0, ALU.mult, ALU.mult)
                elif k == 2:
                    link(dve.tensor_copy(LT, bank[0:R, 6, 0:R]))
                    last = dve.tensor_tensor(ET, LT, eye1, ALU.add)
                elif k < 9:
                    if k < 8:
                        dve.tensor_copy(L, bank[0:R, 6, 0:R])
                        last = dve.tensor_copy(LT, bank[0:R, 6, R:2 * R])
                    if k > 3:
                        last = dve.tensor_tensor(ET, ET, bank[0:R, 6, 2 * R:3 * R], ALU.add)
                elif k == 9:
                    last = dve.tensor_scalar(Xq, bank[0:R, 6, 0:R], -1.0, None, ALU.mult)
                elif k == 10:
                    dve.tensor_copy(U_q, bank[0:KP, 6, 0:KB * R].rearrange("p (a j) -> p a j", a=KB))
                    dve.tensor_tensor(XT[:], XT[:], eye_q, ALU.subtract)
                    link(dve.tensor_copy(QT, bank[:, 7, 0:D]))
                    dve.tensor_tensor(U_q[:, 0, :], U_q[:, 0, :], ident[0:KP, 0:R], ALU.add)
                    last = dve.tensor_tensor(QT[:, 0:R], QT[:, 0:R], eye2[:], ALU.add)
                else:
                    b = (k - 11) * Q4
                    last = dve.tensor_copy(rot_out[:, b:b + Q4, :], bank[0:R, 4:4 + Q4, 0:D])
                last.then_inc(S["fac_out"], 1)

            def norm_stats(n, w, x, stat_sem, mv_sem):
                for tt in range(NT):
                    if w == 0:
                        by_register(dve, S["xa_in"], (n + 1) * 16, S["passed"])
                    else:
                        by_register(dve, S["x2_out"], n * NT + tt + 1, S["passed"])
                    dve.bn_stats(stats[:, tt, :], x[:, tt, :]).then_inc(stat_sem, 1)
                for tt in range(NT):
                    by_register(dve, stat_sem, n * NT + tt + 1, S["passed"])
                    dve.bn_aggr(mv[:, w, tt, :], stats[:, tt, :]).then_inc(mv_sem, 1)

            def norm_apply(n, w, x, rstd_sem, out_sem):
                dve.wait_ge(rstd_sem, n + 1)
                for tt in range(NT):
                    dve.tensor_scalar(xn[:, tt, :], x[:, tt, :], mv[:, w, tt, 0:1], rstd[:, w, tt:tt + 1],
                                      ALU.subtract, ALU.mult).then_inc(out_sem, 1)

            def h32_of(n, kb, bk, m, out_sem):
                col = bass.ds(n, 1)
                dve.tensor_scalar(h32[:, kb, :], bank[0:KP, bk + kb // 2, kb % 2 * N:kb % 2 * N + N],
                                  mod[:, (m + 1) * KB + kb, col], mod[:, m * KB + kb, col],
                                  ALU.mult, ALU.add).then_inc(out_sem, 1)

            def h1(n):
                dve.wait_ge(S["t1_pe"], n + 1)
                for kb in range(KB):
                    h32_of(n, kb, 0, 0, S["h32_1"])

            def h1_low(n):
                for kb in range(KB):
                    dve.wait_ge(S["hhi1"], n * KB + kb + 1)
                    dve.tensor_tensor(h1_lo[:, kb, :], h32[:, kb, :], h1_hi[:, kb, :].bitcast(f32),
                                      ALU.subtract).then_inc(S["h1_out"], 1)

            def h2(n):
                dve.wait_ge(S["t2_pe"], n + 1)
                for kb in range(KB):
                    h32_of(n, kb, 4, 2, S["h32_2"])

            def h2_low(n):
                for kb in range(KB):
                    dve.wait_ge(S["hhi2"], n * KB + kb + 1)
                    dve.tensor_tensor(h2_lo[:, kb, :], h32[:, kb, :], h2_hi[:, kb, :].bitcast(f32),
                                      ALU.subtract).then_inc(S["h2_out"], 1)

            def qk_low(n, i):
                nh = HEADS[i // 2]
                dve.wait_ge(S["qk_hi_out"], n * 6 + i + 1)
                dve.scalar_tensor_tensor(qk_lo[0:nh * HD, i, :], bank[0:nh * HD, 2 + i % 4, 0:N],
                                         bqk[0:nh * HD, i:i + 1], qk_hi[0:nh * HD, i, :].bitcast(f32),
                                         ALU.add, ALU.subtract).then_inc(S["qk_lo_out"], 1)

            def v_out(n):
                for tt in range(NT):
                    dve.wait_ge(S["v_pe"], n * NT + tt + 1)
                    dve.tensor_tensor(v_aug[:, tt, :, 0:HD], bank[:, tt, 0:D].rearrange("p (h d) -> p h d", d=HD),
                                      bv[:].rearrange("p (h d) -> p h d", d=HD), ALU.add).then_inc(S["v_out"], 1)

            def row_max(n, h):
                dve.wait_ge(S["max_pe"], n * H + h + 1)
                dve.tensor_reduce(rowmax[:, :, h], bank[:, 4 + h % 2, :].rearrange("p (t m) -> p t m", t=NT),
                                  AX.X, ALU.max).then_inc(S["max_out"], 1)

            def neg_max(n):
                dve.wait_ge(S["maxt_pe"], n + 1)
                at_least(dve, S["nm_in"], n * 32)
                dve.tensor_scalar(nm_hi[:], bank[0:H, 7, 0:N], -1.0, None, ALU.mult).then_inc(S["nmhi_out"], 1)
                dve.wait_ge(S["nmhi_out"], n + 1)
                dve.scalar_tensor_tensor(nm_lo[:], bank[0:H, 7, 0:N], -1.0, nm_hi[:].bitcast(f32), ALU.mult,
                                         ALU.subtract).then_inc(S["nm_out"], 1)

            def inverse(n, g):
                dve.wait_ge(S["sums_pe"], n * HG + (g + 1))
                dve.reciprocal(o_inv[:, g % 2].rearrange("p t j -> p (t j)"),
                               bank[:, 6 + g % 2, N:N + NT * GH]).then_inc(S["inv_out"], 1)

            def normalize(n, g):
                dve.wait_ge(S["bc_pe"], n * HG + (g + 1))
                dve.tensor_tensor(o_nrm[:, g, :], o_raw[:, g % 2, :], bank[:, 6 + g % 2, N:2 * N],
                                  ALU.mult).then_inc(S["nrm_out"], 1)

            def x2(n):
                dve.wait_ge(S["gate_in"], (n + 1) * 16)
                dve.wait_ge(S["xb_in"], (n + 1) * 16)
                for tt in range(NT):
                    dve.wait_ge(S["proj_pe"], n * NT + tt + 1)
                    dve.tensor_tensor(gated[:, tt, :], bank[:, tt, 0:D], gate_bc[:, 0:D], ALU.mult).then_inc(S["gated1"], 1)
                    dve.wait_ge(S["gated1"], n * NT + tt + 1)
                    dve.tensor_tensor(xb[:, tt, :], xb[:, tt, :], gated[:, tt, :], ALU.add).then_inc(S["x2_out"], 1)
                    by_register(dve, S["x2_out"], n * NT + tt + 1, S["passed"])
                    dve.bn_stats(stats[:, tt, :], xb[:, tt, :]).then_inc(S["stat2"], 1)
                for tt in range(NT):
                    by_register(dve, S["stat2"], n * NT + tt + 1, S["passed"])
                    dve.bn_aggr(mv[:, 1, tt, :], stats[:, tt, :]).then_inc(S["mv2"], 1)

            def x3(n):
                dve.wait_ge(S["fc2k_pe"], (n + 1) * FT)
                dve.wait_ge(S["x2b_out"], n + 1)
                for tt in range(NT):
                    dve.tensor_tensor(gated[:, tt, :], bank[:, tt, 0:D], gate_bc[:, D:2 * D], ALU.mult).then_inc(S["gated2"], 1)
                for tt in range(NT):
                    dve.wait_ge(S["gated2"], n * NT + tt + 1)
                    dve.tensor_tensor(xb[:, tt, :], xb[:, tt, :], gated[:, tt, :], ALU.add).then_inc(S["x3_out"], 1)

            def attention(n, last_attention):
                if not last_attention:
                    norm_stats(n + 1, 0, xa, S["stat1"], S["mv1"])
                qr_first(n, 4)
                if not last_attention:
                    norm_apply(n + 1, 0, xa, S["rstd1"], S["xn1"])
                qr_second(n, 4)
                if not last_attention:
                    h1(n + 1)
                qr_first(n, 5)
                inverse(n, 0)
                qr_second(n, 5)
                normalize(n, 0)
                if not last_attention:
                    h1_low(n + 1)
                inverse(n, 1)
                normalize(n, 1)
                qr_first(n, 6)
                inverse(n, 2)
                qr_second(n, 6)
                normalize(n, 2)
                inverse(n, 3)

            def step(i, last_attention):
                n = i + 1
                normalize(i, 3)
                qk_low(n, 0)
                qk_low(n, 1)
                qr_first(i, 7)
                qr_second(i, 7)
                x2(i)
                qk_low(n, 2)
                norm_apply(i, 1, xb, S["rstd2"], S["xn2"])
                qk_low(n, 3)
                qr_first(n, 0)
                qk_low(n, 4)
                qk_low(n, 5)
                h2(i)
                h2_low(i)
                v_out(n)
                qr_second(n, 0)
                for h in range(H):
                    row_max(n, h)
                    if h in (1, 6, 11):
                        qr_first(n, 1 + h // 5)
                    if h in (3, 8, 12):
                        qr_second(n, 1 + h // 5)
                    if h in (4, 9):
                        square(i * PER_SAMPLE_SQ + h // 5)
                neg_max(n)
                square(i * PER_SAMPLE_SQ + 2)
                x3(i)
                attention(n, last_attention)

            dve.memset(ones_r[:].bitcast(f32), 1.0).then_inc(S["ones_set"], 1)
            norm_stats(0, 0, xa, S["stat1"], S["mv1"])
            def modulation(m0, done):
                dve.wait_ge(S[done], 1)
                rows = slice(m0 * KB, (m0 + 2) * KB)
                link(dve.tensor_tensor(mod[:, rows, :],
                                       bank[0:KP, 2 + m0 // 2, m0 * KB * B:(m0 + 2) * KB * B]
                                       .rearrange("p (m b) -> p m b", b=B),
                                       bada[:, rows].unsqueeze(2).to_broadcast([KP, 2 * KB, B]), ALU.add))
                scale = mod[:, (m0 + 1) * KB:(m0 + 2) * KB, :]
                link(dve.tensor_scalar(scale, scale, 1.0, None, ALU.add))

            norm_apply(0, 0, xa, S["rstd1"], S["xn1"])
            dve.wait_ge(S["wada_in"], 32)
            modulation(0, "ada_pe")
            h1(0)
            split_low(raw_qkv, wqkv_hi, wqkv_lo, "hi_qkv", "lo_qkv")
            h1_low(0)
            dve.wait_ge(S["wada_rest"], 32)
            modulation(2, "adab_pe")
            dve.wait_ge(S["gates_pe"], 1)
            dve.tensor_tensor(gates[:].rearrange("p (g d) -> p g d", g=2), bank[0:B, 4:6, 0:D],
                              gates[:].rearrange("p (g d) -> p g d", g=2), ALU.add).then_inc(S["gates_out"], 1)
            split_low(raw_fc1, wfc1_hi, wfc1_lo, "hi_fc1", "split_out")
            dve.wait_ge(S["consts"], 16 * N_CONSTS)
            dve.wait_ge(S["ident_in"], 16)
            dve.wait_ge(S["pool_set"], 1)
            dve.tensor_copy(e_j[:], ident[0:KP, 0:1]).then_inc(S["pivot_out"], 1)
            split_low(raw_fc2, wfc2_hi, wfc2_lo, "hi_fc2", "split_out")
            dve.wait_ge(S["split_out"], 2)
            dve.memset(v_aug[:], 1.0).then_inc(S["setup_done"], 1)
            dve.wait_ge(S["setup_done"], 1)
            dve.wait_ge(S["bias_in"], 16 * 5)
            qk_low(0, 0)
            qk_low(0, 1)
            qr_first(0, 0)
            qk_low(0, 2)
            qr_second(0, 0)
            for k in range(3, 6):
                qk_low(0, k)
            skew_bias()
            exp_round(0)
            v_out(0)
            for k in range(1, EXP_ROUNDS):
                exp_round(k)
                if k in (3, 5, 7):
                    qr_first(0, k // 2)
                if k in (4, 6, 8):
                    qr_second(0, k // 2 - 1)
                for h in FIRST_MAX_HEADS[k]:
                    row_max(0, h)
            neg_max(0)
            attention(0, False)
            with dve.Fori(0, B - 2) as i:
                step(i, False)
            step(B - 2, True)
            n = B - 1
            normalize(n, 3)
            qr_first(n, 7)
            qr_second(n, 7)
            reflectors()
            x2(n)
            factor(0)
            norm_apply(n, 1, xb, S["rstd2"], S["xn2"])
            h2(n)
            h2_low(n)
            factor(1)
            for k in range(2, FACTOR_ROUNDS - 1):
                factor(k)
            x3(n)
            factor(FACTOR_ROUNDS - 1)
            def x3_turned(n):
                dve.wait_ge(S["t3_pe"], n + 1)
                if n >= 2:
                    dve.wait_ge(S["z_pe"], n - 1)
                dve.tensor_copy(x3T[n % 2][:, 0:2, :].rearrange("p a n -> p (a n)"),
                                bank[0:KP, 2 * (n % 2), :]).then_inc(S["x3t_out"], 1)

            x3_turned(0)
            x3_turned(1)
            for n in range(B):
                if n + 2 < B:
                    x3_turned(n + 2)
                for tt in range(NT):
                    dve.wait_ge(S["rot_pe"], n * NT + tt + 1)
                    if n >= 2:
                        dve.wait_ge(y_stored[n % 2], n // 2 * 16)
                    dve.tensor_tensor(y_sb[n % 2][:, tt, :], x_fin[n][:, tt, :], bank[:, 6 + tt, 0:D],
                                      ALU.add).then_inc(S["y_out"], 1)


def layouts(a):
    def blocks(w, p=KP):
        w = np.asarray(w)
        return np.ascontiguousarray(w.reshape(-1, p, w.shape[-1]).transpose(1, 0, 2))

    f = np.float32
    o = {}
    o["x"] = np.ascontiguousarray(np.asarray(a["x"]).reshape(B, NT, P128, D).transpose(0, 2, 1, 3))
    o["condT"] = blocks(np.asarray(a["cond_1152"]).T)
    o["w_ada"] = blocks(a["L0_cond_w_ada"])
    b_ada = np.asarray(a["L0_cond_b_ada"]).reshape(6, KB, KP)
    o["b_ada"] = np.ascontiguousarray(b_ada[[KIND[m] for m in MOD]].reshape(-1, KP).T)
    gate = np.concatenate([b_ada[KIND["gate_a"]].reshape(-1), b_ada[KIND["gate_f"]].reshape(-1)])
    o["b_gate"] = np.ascontiguousarray(np.stack([gate] * B))
    order = []
    for qk in range(2):
        for i, nh in enumerate(HEADS):
            h0 = sum(HEADS[:i])
            order += [qk * D + (h0 + h) * HD + d for d in range(HD) for h in range(nh)]
    w_qkv = np.asarray(a["L0_cond_w_qkv"])
    o["w_qkv"] = blocks(np.concatenate([w_qkv[:, order], w_qkv[:, 2 * D:]], axis=1))
    b_qkv = np.asarray(a["L0_cond_b_qkv"])
    b_qk = np.zeros((P128, 6), f)
    for i in range(6):
        h0, nh = sum(HEADS[:i // 2]), HEADS[i // 2]
        c = i % 2 * D + h0 * HD
        b_qk[:nh * HD, i] = b_qkv[order[c:c + nh * HD]]
    o["b_qk"] = b_qk
    o["b_v"] = np.ascontiguousarray(b_qkv[2 * D:])
    w_proj = np.zeros((HG, GH, 32, D), f)
    w_proj[:, :, :HD] = np.asarray(a["L0_cond_w_proj"]).reshape(HG, GH, HD, D)
    w_proj[0, 0, HD] = np.asarray(a["L0_cond_b_proj"])
    o["w_proj"] = blocks(w_proj.reshape(HG * P128, D), P128)
    o["w_fc1"] = blocks(a["L0_cond_w_fc1"])
    o["b_fc1"] = np.ascontiguousarray(np.asarray(a["L0_cond_b_fc1"]).reshape(FT, P128).T)
    o["w_fc2"] = blocks(a["L0_cond_w_fc2"], P128)
    o["b_fc2"] = np.ascontiguousarray(np.asarray(a["L0_cond_b_fc2"]))
    o["PT"] = np.concatenate([np.asarray(a["L1_cond_P"]).T, np.zeros((KP - R, D), f)])
    iu, ju = np.triu_indices(R, k=1)
    w = np.zeros((D, R, R), f)
    w[:, iu, ju] = np.asarray(a["L1_cond_W"]).T
    w = [w[:, m:m + TRI, m:].reshape(D, -1) for m in range(0, R, TRI)]
    o["w_skew"] = blocks(np.concatenate(w, axis=1))
    b = np.zeros((R, R), f)
    b[iu, ju] = np.asarray(a["L1_cond_b"])
    o["b_skew"] = np.concatenate([b, b])
    o["ident"] = np.eye(P128, dtype=f)
    sel = np.zeros((P128, P128), f)
    for m in range(P128):
        sel[m // 32 * 32 + HD, m] = 1
    o["sel"] = sel
    o["striu"] = np.triu(np.ones((R, R), f), 1)
    o["eye2"] = np.concatenate([np.eye(R, dtype=f), np.eye(R, dtype=f)])
    o["below"] = -np.tril(np.ones((R, R), f), -1)
    o["upto"] = np.triu(np.ones((R, R), f))
    o["thr"] = np.tile((2.0 ** np.arange(SQUARINGS)).astype(f), (P128, 1))
    return o


def kernel(**inputs):
    import concourse.bacc as bacc
    from concourse.bass_utils import run_bass_kernel_spmd

    arrays = layouts(inputs)
    nc = bacc.Bacc("TRN2", target_bir_lowering=False, num_devices=1)
    t = {n: nc.dram_tensor("in_" + n, a.shape, mybir.dt.from_np(a.dtype), kind="ExternalInput").ap() for n, a in arrays.items()}
    t["y"] = nc.dram_tensor("y", (B, P128, NT, D), mybir.dt.float32, kind="ExternalOutput").ap()
    build(nc, t)
    r = run_bass_kernel_spmd(nc, [{"in_" + n: a for n, a in arrays.items()}], core_ids=[0])
    y = r.results[0]["y"]
    return np.ascontiguousarray(y.transpose(0, 2, 1, 3)).reshape(B, N, D)
```
